# Optimizing a Trainium2 kernel written in Bass

```python
import numpy as np
import jax
import jax.numpy as jnp

def _softmax(x, axis=-1):
    return jax.nn.softmax(x, axis=axis)

def _gelu(x):
    return jax.nn.gelu(x, approximate=True)

def _silu(x):
    return jax.nn.silu(x)

def _sigmoid(x):
    return jax.nn.sigmoid(x)

def _layernorm(x, axis=-1, eps=1e-05):
    m = jnp.mean(x, axis=axis, keepdims=True)
    v = jnp.var(x, axis=axis, keepdims=True)
    return (x - m) / jnp.sqrt(v + eps)

def _scatter_add(tgt, idx, src, axis=0):
    return tgt.at[idx].add(src)

def _segment_sum(src, seg, n):
    return jax.ops.segment_sum(src, seg, n)
kernel_name = 'mk_xattn_seq_d1_seqx_r2_9a43aa'

def setup_inputs(seed: int=0):
    np.random.seed(seed)
    _w = jnp.asarray

    def _rec_inputs():
        import jax
        import jax.numpy as jnp
        _rk = jax.random.key(seed)
        x = 7.22e-05 + 1 * jax.random.normal(jax.random.fold_in(_rk, 1), (8, 512, 1024), jnp.float32)
        _lenS = 512 - jax.random.randint(jax.random.fold_in(_rk, 7), (8,), 0, max(1, 512 // 4) + 1, jnp.int32)
        _lenS2 = 512 - jax.random.randint(jax.random.fold_in(_rk, 8), (8,), 0, max(1, 512 // 4) + 1, jnp.int32)
        _ctx_2048P = jax.random.normal(jax.random.fold_in(_rk, 11), (8, 16, 1024), jnp.float32)
        _ctx_2048c = jax.random.dirichlet(jax.random.fold_in(_rk, 511), 0.3 * jnp.ones((16,), jnp.float32), (8, 512))
        _ctx_2048t = jnp.einsum('bsk,bkd->bsd', _ctx_2048c, _ctx_2048P)
        _ctx_2048t = _ctx_2048t * jax.lax.rsqrt(jnp.mean(jnp.square(_ctx_2048t)) + 1e-12) * 0.953939
        ctx_2048 = 4.13588e-05 + 0.999923 * (_ctx_2048t + 0.3 * jax.random.normal(jax.random.fold_in(_rk, 611), (8, 512, 1024), jnp.float32))
        _validS = jnp.arange(512)[None, :] < _lenS[:, None]
        _validS2 = jnp.arange(512)[None, :] < _lenS2[:, None]
        _causal = jnp.tril(jnp.ones((512, 512), dtype=bool))
        mask_Bx1xSxS2_ff0 = jnp.where(jnp.ones((8, 1, 512, 512), dtype=bool), 0.0, -1000000000.0).astype(jnp.float32)
        return (x, ctx_2048, mask_Bx1xSxS2_ff0)
    x, ctx_2048, mask_Bx1xSxS2_ff0 = _rec_inputs()

    def _L0_xattn_setup():
        import jax, jax.numpy as jnp
        import numpy as np
        H = 1024
        NH = 32
        KVH = 8
        HD = H // NH
        GROUPS = NH // KVH
        EPS = 1e-06
        B, L, S = (4, 512, 512)

        def _gqa_forward(hidden_state, encoder_hidden_state, encoder_attention_mask, Wq, bq, Wk, bk, Wv, bv, Wo, bo, gamma, beta):
            b, l, _ = hidden_state.shape
            s = encoder_hidden_state.shape[1]
            q = hidden_state @ Wq + bq
            k = encoder_hidden_state @ Wk + bk
            v = encoder_hidden_state @ Wv + bv
            q = q.reshape(b, l, KVH, GROUPS, HD).transpose(0, 2, 3, 1, 4)
            k = k.reshape(b, s, KVH, HD).transpose(0, 2, 1, 3)
            v = v.reshape(b, s, KVH, HD).transpose(0, 2, 1, 3)
            scale = 1.0 / jnp.sqrt(jnp.asarray(HD, q.dtype))
            scores = jnp.einsum('bkgld,bksd->bkgls', q, k) * scale
            scores = scores + encoder_attention_mask[:, :, None, :, :]
            attn = jax.nn.softmax(scores, axis=-1)
            out = jnp.einsum('bkgls,bksd->bkgld', attn, v)
            out = out.transpose(0, 3, 1, 2, 4).reshape(b, l, H)
            out = out @ Wo + bo
            x = out + hidden_state
            mu = jnp.mean(x, axis=-1, keepdims=True)
            var = jnp.var(x, axis=-1, keepdims=True)
            return (x - mu) * jax.lax.rsqrt(var + EPS) * gamma + beta
        key = jax.random.key(seed)
        ks = jax.random.split(key, 12)
        sd = 0.02
        return {'hidden_state': jax.random.normal(ks[0], (B, L, H), jnp.float32), 'encoder_hidden_state': jax.random.normal(ks[1], (B, S, H), jnp.float32), 'encoder_attention_mask': jnp.zeros((B, 1, L, S), jnp.float32), 'Wq': jax.random.normal(ks[2], (H, H), jnp.float32) * sd, 'bq': jnp.zeros((H,), jnp.float32), 'Wk': jax.random.normal(ks[3], (H, KVH * HD), jnp.float32) * sd, 'bk': jnp.zeros((KVH * HD,), jnp.float32), 'Wv': jax.random.normal(ks[4], (H, KVH * HD), jnp.float32) * sd, 'bv': jnp.zeros((KVH * HD,), jnp.float32), 'Wo': jax.random.normal(ks[5], (H, H), jnp.float32) * sd, 'bo': jnp.zeros((H,), jnp.float32), 'gamma': jnp.ones((H,), jnp.float32), 'beta': jnp.zeros((H,), jnp.float32)}
    _L0_xattn_all = _L0_xattn_setup()
    _L0_xattn_in = {k: v for k, v in _L0_xattn_all.items() if k in ('Wq', 'bq', 'Wk', 'bk', 'Wv', 'bv', 'Wo', 'bo', 'gamma', 'beta')}
    del _L0_xattn_all
    return {'x': x, 'ctx_2048': ctx_2048, 'mask_Bx1xSxS2_ff0': mask_Bx1xSxS2_ff0, 'L0_xattn_Wq': _L0_xattn_in['Wq'], 'L0_xattn_bq': _L0_xattn_in['bq'], 'L0_xattn_Wk': _L0_xattn_in['Wk'], 'L0_xattn_bk': _L0_xattn_in['bk'], 'L0_xattn_Wv': _L0_xattn_in['Wv'], 'L0_xattn_bv': _L0_xattn_in['bv'], 'L0_xattn_Wo': _L0_xattn_in['Wo'], 'L0_xattn_bo': _L0_xattn_in['bo'], 'L0_xattn_gamma': _L0_xattn_in['gamma'], 'L0_xattn_beta': _L0_xattn_in['beta']}

def reference(x, ctx_2048, mask_Bx1xSxS2_ff0, L0_xattn_Wq, L0_xattn_bq, L0_xattn_Wk, L0_xattn_bk, L0_xattn_Wv, L0_xattn_bv, L0_xattn_Wo, L0_xattn_bo, L0_xattn_gamma, L0_xattn_beta):
    import jax
    import jax.numpy as jnp

    def _L0_xattn_ref(hidden_state, encoder_hidden_state, encoder_attention_mask, Wq, bq, Wk, bk, Wv, bv, Wo, bo, gamma, beta):
        import jax, jax.numpy as jnp
        import numpy as np
        H = 1024
        NH = 32
        KVH = 8
        HD = H // NH
        GROUPS = NH // KVH
        EPS = 1e-06
        B, L, S = (4, 512, 512)

        def _gqa_forward(hidden_state, encoder_hidden_state, encoder_attention_mask, Wq, bq, Wk, bk, Wv, bv, Wo, bo, gamma, beta):
            b, l, _ = hidden_state.shape
            s = encoder_hidden_state.shape[1]
            q = hidden_state @ Wq + bq
            k = encoder_hidden_state @ Wk + bk
            v = encoder_hidden_state @ Wv + bv
            q = q.reshape(b, l, KVH, GROUPS, HD).transpose(0, 2, 3, 1, 4)
            k = k.reshape(b, s, KVH, HD).transpose(0, 2, 1, 3)
            v = v.reshape(b, s, KVH, HD).transpose(0, 2, 1, 3)
            scale = 1.0 / jnp.sqrt(jnp.asarray(HD, q.dtype))
            scores = jnp.einsum('bkgld,bksd->bkgls', q, k) * scale
            scores = scores + encoder_attention_mask[:, :, None, :, :]
            attn = jax.nn.softmax(scores, axis=-1)
            out = jnp.einsum('bkgls,bksd->bkgld', attn, v)
            out = out.transpose(0, 3, 1, 2, 4).reshape(b, l, H)
            out = out @ Wo + bo
            x = out + hidden_state
            mu = jnp.mean(x, axis=-1, keepdims=True)
            var = jnp.var(x, axis=-1, keepdims=True)
            return (x - mu) * jax.lax.rsqrt(var + EPS) * gamma + beta
        return _gqa_forward(hidden_state, encoder_hidden_state, encoder_attention_mask, Wq, bq, Wk, bk, Wv, bv, Wo, bo, gamma, beta)
    x = _L0_xattn_ref(x, ctx_2048, mask_Bx1xSxS2_ff0, L0_xattn_Wq, L0_xattn_bq, L0_xattn_Wk, L0_xattn_bk, L0_xattn_Wv, L0_xattn_bv, L0_xattn_Wo, L0_xattn_bo, L0_xattn_gamma, L0_xattn_beta)
    return x

_drawn_inputs = setup_inputs


def setup_inputs(seed=0):
    import zlib

    import numpy as np

    out = dict(_drawn_inputs(seed))
    spreads = {'L0_xattn_bq': (0.0, 0.8),
     'L0_xattn_bk': (0.0, 2.0),
     'L0_xattn_bv': (0.0, 0.1),
     'L0_xattn_bo': (0.0, 0.1),
     'L0_xattn_gamma': (1.0, 0.2),
     'L0_xattn_beta': (0.0, 0.1)}
    factors = {}
    for name, (base, spread) in spreads.items():
        noise = np.random.default_rng([zlib.crc32(name.encode()), seed]).standard_normal(out[name].shape)
        drawn = base * np.exp(spread * noise) if base else spread * noise
        out[name] = jnp.asarray(drawn.astype(out[name].dtype))
    for name, factor in factors.items():
        out[name] = (out[name] * factor).astype(out[name].dtype)
    return out
```

```python
from contextlib import ExitStack

import concourse.bass as bass
from concourse import mybir

F32 = mybir.dt.float32
F32R = mybir.dt.float32r
ALU = mybir.AluOpType
ACT = mybir.ActivationFunctionType

P = 128
LOWEST = -3.4028234e38




def timeline(g, project, last):
    at = []

    def put(pos, *entry):
        at.append((pos, len(at), entry))

    more = not (last and g == 7)
    p2_at, p1_at = [], []
    pos = 0
    for _ in range(6):
        p2_at.append(pos)
        pos += 1
    for n in range(21):
        (p2_at if n % 4 == 3 else p1_at).append(pos)
        pos += 1
    for _ in range(5):
        p2_at.append(pos)
        pos += 1
    for i, x in enumerate(p2_at):
        put(x, "p2", i)
    if more:
        put(-0.5, "load_stack")
        for i, x in enumerate(p1_at):
            put(x, "p1", i)
        put(p1_at[-1] + 0.4, "shift_neg")
        put(29.5, "shift_turn")
        put(30.5, "shift_out")
    put(p2_at[1] + 0.1, "pv_before")
    put(p2_at[3] + 0.1, "out_group")
    for st in range(3):
        put(p2_at[4 * st + 5] + 0.1, "pv", st)
    if g == 0:
        for j in range(2):
            put(1.3 + j, "v_turn", j)
            put(2.2 + j, "v_out", j)
        for st in (2, 3):
            put(6.6 + 2 * (st - 2), "mask_turn", st)
            put(7.6 + 2 * (st - 2), "mask_out", st)
    if g == 7 and more:
        put(-0.7, "load_mask")
        for st in (0, 1):
            put(14.6 + 4 * st, "mask_turn", st)
            put(16.6 + 4 * st, "mask_out", st)
    if project and g in (0, 3):
        src = g // 3
        first = 11.0 if g == 0 else 1.0
        gap = (31.0 - first - 3) / 8
        for d in range(2):
            put(-0.4, "x_load", src, d)
        for d in range(8):
            x = first + gap * d
            put(x, "x_turn", src, d)
            if d + 2 < 8:
                put(x + 0.01, "x_load", src, d + 2)
            put(x + 1.2, "x_hi", src, d)
            put(x + 1.9, "x_lo", src, d)
    if project and g in (1, 2, 4, 5, 6, 7):
        j0 = 2 * (g - 1) if g < 3 else 4 + 2 * (g - 4)
        for a in range(2):
            m = j0 + a
            for n in range(12):
                put(16 * a + n + 0.5, "mm", m, 2 * n, 2 * n + 2)
            kind = "v_keep" if m in (2, 3) else "split"
            put(16 * a + 12.7, kind, m)
            if kind == "split":
                put(16 * a + 14.2, "split_lo", m)
    if last and g in (1, 2, 3, 4):
        for n in range(4):
            put(4.5 + 7 * n, "wo_hi_lo", 4 * (g - 1) + n)
    if last and g == 5:
        put(3.5, "recip", 0)
    return [e for _, _, e in sorted(at, key=lambda x: (x[0], x[1]))]


def prologue():
    at = []
    for src in range(2):
        at += [("x_load", src, 0), ("x_load", src, 1)]
        for d in range(8):
            at.append(("x_turn", src, d))
            if d + 2 < 8:
                at.append(("x_load", src, d + 2))
            at += [("x_hi", src, d), ("x_lo", src, d)]
        if src == 0:
            at.append(("load_mask",))
        for m in (range(4) if src == 0 else range(4, 12)):
            at.append(("mm", m, 0, 24))
            if m in (2, 3):
                at.append(("v_keep", m))
            else:
                at += [("split", m), ("split_lo", m)]
            if m == 4:
                at.append(("load_stack",))
            if m in (5, 6):
                at += [("mask_turn", m - 5), ("mask_out", m - 5)]
            if m >= 7:
                at += [("p1", i) for i in range(4 * (m - 7), min(4 * (m - 6), 16))]
            if m == 10:
                at += [("shift_neg",), ("shift_turn",), ("shift_out",)]
    return at


def attention_kernel(nc, x, ctx, mask, wq, bq, wk, bk, wv, bv, wo, bo, gamma, beta, out):
    B, L, D = x.shape
    S = ctx.shape[1]
    KV = wk.shape[1]
    HD = 32
    NG = KV // HD
    GH = D // KV
    KD = D // P
    LT, ST = L // P, S // P
    SCALE = float(HD) ** -0.5
    EPS = 1e-6
    NB = B
    assert (L, S, GH * HD, NG, KD) == (512, 512, P, 8, 8)

    STEPS = [timeline(g, True, False) for g in range(NG)]
    LAST = [timeline(g, False, True) for g in range(NG)]
    FIRST = prologue()

    def uses(entries, bank):
        got = []
        for e in entries:
            if e[0] == "x_turn" and e[2] % 2 == bank:
                got.append(e)
            if bank == 0 and e[0] == "mm" and e[2] == 0:
                got.append(("mm", e[1]))
            if bank == 1 and e[0] in ("v_turn", "mask_turn"):
                got.append(e)
        return got

    def spare1(steps):
        got = []
        for g, step in enumerate(steps):
            for e in step:
                if e[0] == "shift_turn":
                    got.append(("shift_turn", g))
                else:
                    got += uses([e], 1)
        return got

    BODY0 = [u for step in STEPS for u in uses(step, 0)]
    FIRST0 = uses(FIRST, 0)
    BODY1, LAST1 = spare1(STEPS), spare1(LAST)
    FIRST1 = [("shift_turn", NG - 1) if e[0] == "shift_turn" else e
              for e in FIRST if e[0] == "shift_turn" or uses([e], 1)]
    assert len(BODY0) == len(FIRST0) == 20

    def use0(t, key):
        return FIRST0.index(key) + 1 if isinstance(t, int) and t < 0 else 20 * (t + 1) + BODY0.index(key) + 1

    def use1(t, key):
        if isinstance(t, int) and t < 0:
            return FIRST1.index(key) + 1
        order = LAST1 if isinstance(t, int) and t == NB - 1 else BODY1
        return len(FIRST1) + len(BODY1) * t + order.index(key) + 1

    with ExitStack() as stack:
        def sb(name, shape, dt, where=stack):
            return where.enter_context(nc.sbuf_tensor(name, shape, dt))

        def sem(name):
            return stack.enter_context(nc.semaphore(name))

        def dram(name, shape, dt):
            return nc.dram_tensor(name, shape, dt, kind="Internal").ap()

        q_hi_d = dram("q_hi_d", [NB * NG, P, L], F32)
        q_lo_d = dram("q_lo_d", [NB * NG, P, L], F32)
        k_hi_d = dram("k_hi_d", [NB * 2, P, S], F32)
        k_lo_d = dram("k_lo_d", [NB * 2, P, S], F32)
        o_d = dram("o_d", [NB * NG, P, L], F32)
        r_d = dram("r_d", [NB * NG, GH, L], F32)
        ri_d = dram("ri_d", [NB * NG, GH, L], F32)

        w_hi = sb("w_hi", [P, KD, D + 2 * KV], F32R)
        w_lo = sb("w_lo", [P, KD, D + 2 * KV], F32R)
        xT_hi = sb("xT_hi", [P, KD, L], F32R)
        xT_lo = sb("xT_lo", [P, KD, L], F32R)
        x_raw = sb("x_raw", [P, 2, L], F32)
        ident = sb("ident", [P, P], F32)
        ones = sb("ones", [P, HD], F32)
        bq_c = sb("bq_c", [P, NG], F32)
        bq_s = sb("bq_s", [P, NG], F32)
        bkv_c = sb("bkv_c", [P, 4], F32)
        eps_c = sb("eps_c", [P, 1], F32)
        row_max = sb("row_max", [P, 4 * GH], F32)
        shift = sb("shift", [P, 2 * 4 * GH], F32R)
        shift_rows = sb("shift_rows", [2 * 4 * GH, P], F32R)
        sums = sb("sums", [P, NG * NB * GH * L // P], F32)
        EARLY = NG * (NB - 1) * GH * L // P
        with ExitStack() as first_part:
            def sb1(name, shape, dt):
                return sb(name, shape, dt, first_part)

            mask_l = sb1("mask_l", [P, LT, S], F32)
            mask_s = sb1("mask_s", [P, ST, L], F32)
            probs = sb1("probs", [P, 8, L], F32)
            q_stack = [sb1(f"q_stack{i}", [98, GH, L], F32R) for i in range(2)]
            k_stack = [sb1(f"k_stack{i}", [98, S], F32R) for i in range(2)]
            v_sb = sb1("v_sb", [P, ST, KV], F32)
            vT_sb = sb1("vT_sb", [P, 2, S], F32)
            part_hi = sb1("part_hi", [P, L], F32R)
            part_lo = sb1("part_lo", [P, L], F32R)
            o_sb = sb1("o_sb", [P, L], F32)
            r_sb = sb1("r_sb", [P, L], F32)
        o_raw = sb("o_raw", [P, 4, L], F32)
        r_inv = sb("r_inv", [P, 4, L], F32)
        x_res = sb("x_res", [P, 2, D], F32)
        y_sb = sb("y_sb", [P, 2, D], F32)
        z_sb = sb("z_sb", [P, 2, D], F32)
        bo_b = sb("bo_b", [P, D], F32)
        gamma_b = sb("gamma_b", [P, D], F32)
        beta_b = sb("beta_b", [P, D], F32)
        stats = sb("stats", [P, 2, 6], F32)
        mean_var = sb("mean_var", [P, 2], F32)
        std = sb("std", [P, 1], F32)
        rstd = sb("rstd", [P, 1], F32)

        bank = [stack.enter_context(nc.psum_tensor(f"bank{i}", [P, 512], F32)) for i in range(8)]
        S1, S2, O_ps, R_ps, C = bank[0:2], bank[2:4], bank[4], bank[5], bank[6:8]
        Y = bank[0:4]

        consts_ready = sem("consts_ready")
        biases_in = sem("biases_in")
        bias_scaled = sem("bias_scaled")
        w_in = [sem(f"w_in{i}") for i in range(8)]
        w_hi_done, w_lo_done = sem("w_hi_done"), sem("w_lo_done")
        x_in = [sem("x_in0"), sem("x_in1")]
        c_full = [sem("c_full0"), sem("c_full1")]
        c_free = [sem("c_free0"), sem("c_free1")]
        hi_done = sem("hi_done")
        biased = sem("biased")
        qk_stored = sem("qk_stored")
        mask_in = sem("mask_in")
        stack_in = sem("stack_in")
        p1_done, max_done = sem("p1_done"), sem("max_done")
        neg_hi, neg_lo = sem("neg_hi"), sem("neg_lo")
        shift_in = sem("shift_in")
        p2_done, masked, exp_done = sem("p2_done"), sem("masked"), sem("exp_done")
        pv_done = sem("pv_done")
        o_out, o_stored = sem("o_out"), sem("o_stored")
        wo_in = [sem("wo_in0"), sem("wo_in1")]
        wo_hi_done, wo_lo_done = sem("wo_hi_done"), sem("wo_lo_done")
        r_in, r_done, ri_stored = sem("r_in"), sem("r_done"), sem("ri_stored")
        rows_in = sem("rows_in")
        o_in = [sem(f"o_in{i}") for i in range(4)]
        normed, on_hi, on_lo = sem("normed"), sem("on_hi"), sem("on_lo")
        res_in = [sem("res_in0"), sem("res_in1")]
        res_bo = sem("res_bo")
        y_full, y_added = sem("y_full"), sem("y_added")
        y_stat, y_mv, y_std, y_rstd, y_cen = (sem(n) for n in ("y_stat", "y_mv", "y_std", "y_rstd", "y_cen"))
        z_done = sem("z_done")
        z_stored = [sem("z_stored0"), sem("z_stored1")]

        HI_PER_BATCH = 16 + 2 + 8
        HI_ORDER = [e for e in FIRST if e[0] in ("x_hi", "split")]
        assert HI_ORDER == [e for step in STEPS for e in step if e[0] in ("x_hi", "split")]
        SPLITS = [e[1] for e in HI_ORDER if e[0] == "split"]

        def hi_no(t, e):
            return HI_PER_BATCH * (t + 1) + HI_ORDER.index(e) + 1

        def split_no(t, m):
            return 10 * (t + 1) + SPLITS.index(m) + 1

        def wait(eng, s, value):
            if not (isinstance(value, int) and value <= 0):
                eng.wait_ge(s, value)

        def walk(eng, do):
            for e in FIRST:
                do(-1, NG - 1, e)
            for g in range(NG):
                for e in STEPS[g]:
                    do(0, g, e)
            with eng.Fori(1, NB - 1) as t:
                for g in range(NG):
                    for e in STEPS[g]:
                        do(t, g, e)
            for g in range(NG):
                for e in LAST[g]:
                    do(NB - 1, g, e)

        def group(t, g):
            return NG * t + g

        def use_c(t, c, key):
            return use0(t, key) if c == 0 else use1(t, key)

        def use_of_turn(t, src, d):
            if d >= 2:
                return use_c(t, d % 2, ("x_turn", src, d - 2))
            if src == 1:
                return use_c(t, d % 2, ("x_turn", 0, d + 6))
            if isinstance(t, int) and t < 0:
                return 0
            return use_c(t - 1, d % 2, ("x_turn", 1, d + 6))

        def mask_use(t, st):
            if st < 2:
                return use1(t - 1, ("mask_turn", st))
            return use1(t, ("mask_turn", st))

        def w_place(n):
            return (n // 2, (n % 2) * 512) if n < 16 else (n - 16, D)

        def rows_of(a, part):
            cut = NG * (NB - 1)
            r = (a[0:cut] if part == 0 else a[cut:NG * NB]).rearrange("g h l -> (g h l)")
            return r.rearrange("(p f) -> p f", p=P)

        def halves(odd):
            if odd:
                return w_hi[:, :, D:D + 512], w_lo[:, :, D:D + 512]
            return xT_hi[:, :, :], xT_lo[:, :, :]

        block = stack.enter_context(nc.Block())

        @block.sync
        def _(sp):
            def w_piece(n):
                if n < 16:
                    return [(slice(0, 512), wq[(n // 2) * P:(n // 2 + 1) * P, (n % 2) * 512:(n % 2 + 1) * 512])]
                k = n - 16
                return [(slice(0, KV), wk[k * P:(k + 1) * P, :]), (slice(KV, 2 * KV), wv[k * P:(k + 1) * P, :])]

            order = list(range(16, 24)) + list(range(16))
            for k, n in enumerate(order):
                if k >= 8:
                    sp.wait_ge(w_lo_done, k - 7)
                for cols, src in w_piece(n):
                    sp.dma_start(probs[:, k % 8, cols], src).then_inc(w_in[k % 8], 16)
                if k == 0:
                    with nc.allow_non_contiguous_dma(reason="bias columns, once"):
                        sp.dma_start(bq_c[:, :], bq.rearrange("(g p) -> p g", p=P)).then_inc(biases_in, 16)
                        sp.dma_start(bkv_c[:, 0:2], bk.rearrange("(g p) -> p g", p=P)).then_inc(biases_in, 16)
                        sp.dma_start(bkv_c[:, 2:4], bv.rearrange("(g p) -> p g", p=P)).then_inc(biases_in, 16)

            def do(t, g, e):
                kind = e[0]
                if kind == "x_load":
                    src, d = e[1], e[2]
                    before = use_of_turn(t, src, d)
                    wait(sp, c_full[d % 2], before)
                    dram_in = (ctx, x)[src][t + 1].rearrange("(a p) d -> p a d", p=P)[:, :, d * P:(d + 1) * P]
                    sp.dma_start(x_raw[:, d % 2, :].rearrange("p (a d) -> p a d", a=LT), dram_in)\
                      .then_inc(x_in[d % 2], 16)
                elif kind == "load_mask":
                    wait(sp, max_done, 128 * (t + 1))
                    sp.dma_start(mask_l[:, :, :], mask[t + 1, 0].rearrange("(a p) s -> p a s", p=P))\
                      .then_inc(mask_in, 16)
                elif kind == "split_lo":
                    m = e[1]
                    wait(sp, c_free[0], use0(t, ("mm", m)))
                    hi_dst, lo_dst = (k_hi_d, k_lo_d) if m < 2 else (q_hi_d, q_lo_d)
                    row = 2 * (t + 1) + m if m < 2 else NG * (t + 1) + m - 4
                    sp.dma_start(hi_dst[row], part_hi[:, :].bitcast(F32)).then_inc(qk_stored, 16)
                    sp.dma_start(lo_dst[row], part_lo[:, :].bitcast(F32)).then_inc(qk_stored, 16)
                elif kind == "load_stack":
                    G = group(t, g) + 1
                    b = (g + 1) % 2
                    wait(sp, p2_done, 16 * (G - 1))
                    nt, ng = (t, g + 1) if g + 1 < NG else (t + 1, 0)
                    wait(sp, qk_stored, 32 * split_no(nt - 1, 4 + ng))
                    q_hi, q_lo = (a[G].rearrange("(h d) l -> d h l", h=GH) for a in (q_hi_d, q_lo_d))
                    kr = 2 * nt + ng // 4
                    k0 = HD * (ng % 4)
                    k_hi, k_lo = (a[kr][k0:k0 + HD, :] for a in (k_hi_d, k_lo_d))
                    for i, (q, k) in enumerate(((q_hi, k_hi), (q_lo, k_hi), (q_hi, k_lo))):
                        sp.dma_start(k_stack[b][HD * i:HD * (i + 1), :].bitcast(F32), k).then_inc(stack_in, 16)
                        sp.dma_start(q_stack[b][HD * i:HD * (i + 1), :, :].bitcast(F32), q).then_inc(stack_in, 16)
                elif kind == "shift_out":
                    G = group(t, g) + 1
                    b = (g + 1) % 2
                    wait(sp, c_free[1], use1(t, ("shift_turn", g)))
                    for r in range(2):
                        sp.dma_start(q_stack[b][96 + r:97 + r, :, :].bitcast(F32),
                                     shift_rows[16 * r:16 * (r + 1), :].bitcast(F32)).then_inc(shift_in, 16)
                elif kind == "out_group" and not (isinstance(t, int) and t == 0 and g == 0):
                    store_group(group(t, g) - 1)
                elif kind == "wo_hi_lo":
                    n = e[1]
                    if n >= 2:
                        sp.wait_ge(wo_lo_done, n - 1)
                    sp.dma_start(x_raw[:, n % 2, :], wo[(n // 2) * P:(n // 2 + 1) * P,
                                                        (n % 2) * 512:(n % 2 + 1) * 512]).then_inc(wo_in[n % 2], 16)
                elif kind == "recip":
                    sp.wait_ge(o_stored, 32 * NG * (NB - 1))
                    sp.dma_start(sums[:, 0:EARLY], rows_of(r_d, 0)).then_inc(r_in, 16)
                    sp.wait_ge(r_done, 1)
                    sp.dma_start(rows_of(ri_d, 0), sums[:, 0:EARLY]).then_inc(ri_stored, 16)

            def store_group(G):
                sp.wait_ge(o_out, 2 * (G + 1))
                sp.dma_start(o_d[G], o_sb[:, :]).then_inc(o_stored, 16)
                sp.dma_start(r_d[G], r_sb[0:P:HD, :]).then_inc(o_stored, 16)

            walk(sp, do)
            store_group(NB * NG - 1)

            sp.wait_ge(o_stored, 32 * NG * NB)
            sp.dma_start(sums[:, EARLY:], rows_of(r_d, 1)).then_inc(r_in, 16)
            sp.dma_start(bo_b[:, :], bo.rearrange("(a d) -> a d", a=1).broadcast_to([P, D])).then_inc(rows_in, 16)
            sp.dma_start(gamma_b[:, :], gamma.rearrange("(a d) -> a d", a=1).broadcast_to([P, D])).then_inc(rows_in, 16)
            sp.dma_start(beta_b[:, :], beta.rearrange("(a d) -> a d", a=1).broadcast_to([P, D])).then_inc(rows_in, 16)

            def load_o(b, g):
                n = NG * b + g
                wait(sp, on_lo, n - 3)
                sp.dma_start(o_raw[:, g % 4, :], o_d[n]).then_inc(o_in[g % 4], 16)
                for h in range(GH):
                    sp.dma_start(r_inv[HD * h:HD * (h + 1), g % 4, :],
                                 ri_d[n][h:h + 1, :].broadcast_to([HD, L])).then_inc(o_in[g % 4], 16)

            def load_res(b, lt):
                T = LT * b + lt
                wait(sp, y_added, 2 * (T - 1))
                sp.dma_start(x_res[:, lt % 2, :], x[b, lt * P:(lt + 1) * P, :]).then_inc(res_in[lt % 2], 16)

            def store(b, lt):
                T = LT * b + lt
                sp.wait_ge(z_done, T + 1)
                sp.dma_start(out[b, lt * P:(lt + 1) * P, :], z_sb[:, lt % 2, :]).then_inc(z_stored[lt % 2], 16)

            sp.wait_ge(ri_stored, 16)
            for g in range(NG):
                load_o(0, g)
                if g == 3:
                    load_res(0, 0)
                    load_res(0, 1)
            sp.wait_ge(r_done, 2)
            sp.dma_start(rows_of(ri_d, 1), sums[:, EARLY:]).then_inc(ri_stored, 16)
            sp.wait_ge(ri_stored, 32)

            def batch_rows(b, more):
                for lt in range(LT):
                    if more:
                        load_o(b + 1, 2 * lt)
                        load_o(b + 1, 2 * lt + 1)
                    store(b, lt)
                    if lt + 2 < LT:
                        load_res(b, lt + 2)
                    elif more:
                        load_res(b + 1, lt - 2)

            batch_rows(0, True)
            with sp.Fori(1, NB - 1) as b:
                batch_rows(b, True)
            batch_rows(NB - 1, False)
            sp.wait_ge(z_stored[0], 16 * 2 * NB)
            sp.wait_ge(z_stored[1], 16 * 2 * NB)

        @block.gpsimd
        def _(pool):
            nc.gpsimd.memset(ident[:, :], 0.0).then_inc(consts_ready, 1)
            nc.gpsimd.memset(ones[:, :], 1.0).then_inc(consts_ready, 1)
            nc.gpsimd.memset(eps_c[:, :], EPS).then_inc(consts_ready, 1)
            for i in range(2):
                pool.wait_ge(consts_ready, 3 + i)
                nc.gpsimd.memset(k_stack[i][96:98, :].bitcast(F32), 1.0).then_inc(consts_ready, 1)
            pool.wait_ge(consts_ready, 5)
            nc.gpsimd.affine_select(out=ident[:, :], in_=ident[:, :], compare_op=ALU.not_equal, fill=1.0, base=0,
                                    pattern=[[-1, P]], channel_multiplier=1).then_inc(consts_ready, 1)
            for n in range(16):
                pool.wait_ge(wo_hi_done, n + 1)
                k, c = n // 2, (n % 2) * 512
                nc.gpsimd.tensor_tensor(w_lo[:, k, c:c + 512], x_raw[:, n % 2, :],
                                        w_hi[:, k, c:c + 512].bitcast(F32), ALU.subtract).then_inc(wo_lo_done, 1)

            def lo(b, g, odd):
                n = NG * b + g
                _, d_lo = halves(odd)
                d_hi, _ = halves(odd)
                pool.wait_ge(on_hi, n + 1)
                nc.gpsimd.tensor_tensor(d_lo[:, g, :], o_raw[:, g % 4, :], d_hi[:, g, :].bitcast(F32),
                                        ALU.subtract).then_inc(on_lo, 1)

            def residual(b, lt):
                T = LT * b + lt
                pool.wait_ge(res_in[lt % 2], 16 * (2 * b + lt // 2 + 1))
                nc.gpsimd.tensor_tensor(x_res[:, lt % 2, :], x_res[:, lt % 2, :], bo_b[:, :], ALU.add)\
                  .then_inc(res_bo, 1)

            for g in range(NG):
                lo(0, g, 0)
            pool.wait_ge(rows_in, 48)

            def batch_rows(b, odd, more):
                for lt in range(LT):
                    residual(b, lt)
                    if more:
                        lo(b + 1, 2 * lt, 1 - odd)
                        lo(b + 1, 2 * lt + 1, 1 - odd)

            with pool.Fori(0, NB // 2 - 1) as p:
                batch_rows(2 * p, 0, True)
                batch_rows(2 * p + 1, 1, True)
            batch_rows(NB - 2, 0, True)
            batch_rows(NB - 1, 1, False)

        @block.scalar
        def _(act):
            order = list(range(16, 24)) + list(range(16))
            count = [0] * 8
            for k, n in enumerate(order):
                count[k % 8] += 32 if n >= 16 else 16
                act.wait_ge(w_in[k % 8], count[k % 8])
                d, c = w_place(n)
                nc.scalar.activation(w_hi[:, d, c:c + 512], probs[:, k % 8, :], ACT.Copy).then_inc(w_hi_done, 1)
            act.wait_ge(biases_in, 48)
            nc.scalar.mul(bq_s[:, :], bq_c[:, :], SCALE).then_inc(bias_scaled, 1)
            act.wait_ge(bias_scaled, 1)

            def do(t, g, e):
                kind = e[0]
                if kind == "x_hi":
                    src, d = e[1], e[2]
                    act.wait_ge(c_full[d % 2], use_c(t, d % 2, ("x_turn", src, d)))
                    nc.scalar.activation(xT_hi[:, d, :], C[d % 2][:, :], ACT.Copy).then_inc(hi_done, 1)
                elif kind == "split":
                    m = e[1]
                    act.wait_ge(c_full[0], use0(t, ("mm", m)))
                    n = split_no(t, m)
                    if m < 2:
                        nc.scalar.activation(C[0][:, :], C[0][:, :], ACT.Identity, bias=bkv_c[:, m:m + 1])\
                          .then_inc(biased, 1)
                    else:
                        nc.scalar.activation(C[0][:, :], C[0][:, :], ACT.Identity, scale=SCALE,
                                             bias=bq_s[:, m - 4:m - 3]).then_inc(biased, 1)
                    act.wait_ge(biased, n)
                    wait(act, qk_stored, 32 * (n - 1))
                    nc.scalar.activation(part_hi[:, :], C[0][:, :], ACT.Copy).then_inc(hi_done, 1)
                elif kind == "v_keep":
                    m = e[1]
                    act.wait_ge(c_full[0], use0(t, ("mm", m)))
                    nc.scalar.activation(vT_sb[:, m - 2, :], C[0][:, :], ACT.Identity, bias=bkv_c[:, m:m + 1])\
                      .then_inc(c_free[0], 1)
                elif kind == "v_out":
                    j = e[1]
                    act.wait_ge(c_full[1], use1(t, ("v_turn", j)))
                    wait(act, pv_done, 4 * NG * t)
                    nc.scalar.activation(v_sb[:, :, j * P:(j + 1) * P],
                                         C[1][:, :].rearrange("p (s d) -> p s d", s=ST), ACT.Copy)\
                      .then_inc(c_free[1], 1)
                elif kind == "mask_out":
                    st = e[1]
                    act.wait_ge(c_full[1], use1(t, ("mask_turn", st)))
                    nt = t + 1 if g == 7 else t
                    wait(act, masked, 128 * nt - 16 + 4 * st + 4 if not (isinstance(nt, int) and nt == 0) else 0)
                    nc.scalar.activation(mask_s[:, st, :], C[1][:, :], ACT.Copy).then_inc(c_free[1], 1)
                elif kind == "shift_out":
                    G = group(t, g) + 1
                    act.wait_ge(c_full[1], use1(t, ("shift_turn", g)))
                    wait(act, shift_in, 32 * G)
                    nc.scalar.activation(shift_rows[:, :], C[1][0:32, 0:P], ACT.Copy).then_inc(c_free[1], 1)
                elif kind == "p2":
                    i = e[1]
                    n = 16 * group(t, g) + i
                    act.wait_ge(masked, n + 1)
                    wait(act, pv_done, 4 * group(t, g) + i // 4 - 1)
                    nc.scalar.activation(probs[:, i % 8, :], S2[i % 2][:, :], ACT.Exp).then_inc(exp_done, 1)
                elif kind == "out_group" and not (isinstance(t, int) and t == 0 and g == 0):
                    out_group(group(t, g) - 1)
                elif kind == "wo_hi_lo":
                    n = e[1]
                    act.wait_ge(wo_in[n % 2], 16 * (n // 2 + 1))
                    k, c = n // 2, (n % 2) * 512
                    act.wait_ge(c_full[0], 20 * NB)
                    nc.scalar.activation(w_hi[:, k, c:c + 512], x_raw[:, n % 2, :], ACT.Copy).then_inc(wo_hi_done, 1)

            def out_group(G):
                act.wait_ge(pv_done, 4 * (G + 1))
                wait(act, o_stored, 32 * G)
                nc.scalar.activation(o_sb[:, :], O_ps[:, :], ACT.Copy).then_inc(o_out, 1)
                nc.scalar.activation(r_sb[:, :], R_ps[:, :], ACT.Copy).then_inc(o_out, 1)

            walk(act, do)
            out_group(NB * NG - 1)

            def hi(b, g, odd):
                n = NG * b + g
                d_hi, _ = halves(odd)
                act.wait_ge(normed, n + 1)
                wait(act, y_full, 8 * (b - 1) if not (isinstance(b, int) and b == 0) else 0)
                nc.scalar.activation(d_hi[:, g, :], o_raw[:, g % 4, :], ACT.Copy).then_inc(on_hi, 1)

            def root(b, lt):
                T = LT * b + lt
                act.wait_ge(y_mv, T + 1)
                nc.scalar.activation(std[:, :], mean_var[:, 1:2], ACT.Sqrt, bias=eps_c[:, :]).then_inc(y_std, 1)

            for g in range(NG):
                hi(0, g, 0)

            def batch_rows(b, odd, more):
                for lt in range(LT):
                    if more:
                        hi(b + 1, 2 * lt, 1 - odd)
                        hi(b + 1, 2 * lt + 1, 1 - odd)
                    root(b, lt)

            batch_rows(0, 0, True)
            batch_rows(1, 1, True)
            with act.Fori(1, NB // 2 - 1) as p:
                batch_rows(2 * p, 0, True)
                batch_rows(2 * p + 1, 1, True)
            batch_rows(NB - 2, 0, True)
            batch_rows(NB - 1, 1, False)

        @block.vector
        def _(dve):
            order = list(range(16, 24)) + list(range(16))
            for k, n in enumerate(order):
                dve.wait_ge(w_hi_done, k + 1)
                d, c = w_place(n)
                nc.vector.tensor_tensor(w_lo[:, d, c:c + 512], probs[:, k % 8, :],
                                        w_hi[:, d, c:c + 512].bitcast(F32), ALU.subtract).then_inc(w_lo_done, 1)

            def do(t, g, e):
                kind = e[0]
                if kind == "x_lo":
                    src, d = e[1], e[2]
                    dve.wait_ge(hi_done, hi_no(t, ("x_hi", src, d)))
                    nc.vector.tensor_tensor(xT_lo[:, d, :], C[d % 2][:, :], xT_hi[:, d, :].bitcast(F32),
                                            ALU.subtract).then_inc(c_free[d % 2], 1)
                elif kind == "split_lo":
                    m = e[1]
                    dve.wait_ge(hi_done, hi_no(t, ("split", m)))
                    nc.vector.tensor_tensor(part_lo[:, :], C[0][:, :], part_hi[:, :].bitcast(F32),
                                            ALU.subtract).then_inc(c_free[0], 1)
                elif kind == "p1":
                    i = e[1]
                    n = 16 * (group(t, g) + 1) + i
                    h, lt = i // 4, i % 4
                    if i == 0:
                        dve.wait_ge(mask_in, 16 * (t + 2) if g == 7 else 16 * (t + 1))
                    if not isinstance(n, int):
                        dve.lower_val(n + 1)
                    dve.wait_ge(w_hi_done, 24)
                    dve.wait_ge(p1_done, n + 1)
                    nc.vector.tensor_tensor_reduce(out=S1[i % 2][:, :], in0=S1[i % 2][:, :], in1=mask_l[:, lt, :],
                                                   scale=1.0, scalar=LOWEST, op0=ALU.add, op1=ALU.max,
                                                   accum_out=row_max[:, i:i + 1]).then_inc(max_done, 1)
                elif kind == "shift_neg":
                    G = group(t, g) + 1
                    dve.wait_ge(max_done, 16 * (G + 1))
                    if not (isinstance(t, int) and t < 0):
                        pt, pg = (t, g - 1) if g > 0 else (t - 1, NG - 1)
                        dve.wait_ge(c_full[1], use1(pt, ("shift_turn", pg)))
                    nc.vector.tensor_scalar(shift[:, 0:16], row_max[:, :], -1.0, None, ALU.mult).then_inc(neg_hi, 1)
                    dve.wait_ge(neg_hi, G + 1)
                    nc.vector.scalar_tensor_tensor(out=shift[:, 16:32], in0=row_max[:, :], scalar=-1.0,
                                                   in1=shift[:, 0:16].bitcast(F32), op0=ALU.mult, op1=ALU.subtract)\
                      .then_inc(neg_lo, 1)
                elif kind == "p2":
                    i = e[1]
                    st = i // 4
                    n = 16 * group(t, g) + i
                    if g == 0 and i % 4 == 0:
                        dve.wait_ge(c_free[1], mask_use(t, st))
                    dve.wait_ge(p2_done, n + 1)
                    nc.vector.tensor_tensor(S2[i % 2][:, :], S2[i % 2][:, :], mask_s[:, st, :], ALU.add)\
                      .then_inc(masked, 1)
                elif kind == "recip":
                    dve.wait_ge(r_in, 16)
                    nc.vector.reciprocal(sums[:, 0:EARLY], sums[:, 0:EARLY]).then_inc(r_done, 1)

            walk(dve, do)
            dve.wait_ge(r_in, 32)
            nc.vector.reciprocal(sums[:, EARLY:], sums[:, EARLY:]).then_inc(r_done, 1)

            def norm(b, g):
                n = NG * b + g
                dve.wait_ge(o_in[g % 4], 80 * (2 * b + g // 4 + 1))
                nc.vector.tensor_tensor(o_raw[:, g % 4, :], o_raw[:, g % 4, :], r_inv[:, g % 4, :], ALU.mult)\
                  .then_inc(normed, 1)

            for g in range(NG):
                norm(0, g)

            def rows(b, lt):
                T = LT * b + lt
                i = lt % 2
                dve.wait_ge(res_bo, T + 1)
                for c in range(2):
                    dve.wait_ge(y_full, 2 * T + c + 1)
                    nc.vector.tensor_tensor(y_sb[:, i, c * 512:(c + 1) * 512], Y[2 * i + c][:, :],
                                            x_res[:, i, c * 512:(c + 1) * 512], ALU.add).then_inc(y_added, 1)
                for c in range(2):
                    dve.wait_ge(y_added, 2 * T + c + 1)
                    nc.vector.bn_stats(stats[:, c, :], y_sb[:, i, c * 512:(c + 1) * 512]).then_inc(y_stat, 1)
                dve.wait_ge(wo_hi_done, 16)
                dve.wait_ge(y_stat, 2 * T + 2)
                nc.vector.bn_aggr(mean_var[:, :], stats[:, :, :]).then_inc(y_mv, 1)
                dve.wait_ge(y_mv, T + 1)
                wait(dve, z_stored[i], 16 * (2 * b + lt // 2))
                nc.vector.scalar_tensor_tensor(out=z_sb[:, i, :], in0=y_sb[:, i, :], scalar=mean_var[:, 0:1],
                                               in1=gamma_b[:, :], op0=ALU.subtract, op1=ALU.mult).then_inc(y_cen, 1)
                dve.wait_ge(y_std, T + 1)
                nc.vector.reciprocal(rstd[:, :], std[:, :]).then_inc(y_rstd, 1)
                dve.wait_ge(y_rstd, T + 1)
                dve.wait_ge(y_cen, T + 1)
                nc.vector.scalar_tensor_tensor(out=z_sb[:, i, :], in0=z_sb[:, i, :], scalar=rstd[:, :],
                                               in1=beta_b[:, :], op0=ALU.mult, op1=ALU.add).then_inc(z_done, 1)

            def batch_rows(b, more):
                for lt in range(LT):
                    if more:
                        norm(b + 1, 2 * lt)
                        norm(b + 1, 2 * lt + 1)
                    rows(b, lt)

            batch_rows(0, True)
            with dve.Fori(1, NB - 1) as b:
                batch_rows(b, True)
            batch_rows(NB - 1, False)

        @block.tensor
        def _(pe):
            pe.wait_ge(consts_ready, 6)

            def do(t, g, e):
                kind = e[0]
                if kind == "x_turn":
                    src, d = e[1], e[2]
                    c = d % 2
                    n = use_c(t, c, ("x_turn", src, d))
                    pe.wait_ge(x_in[c], 16 * (8 * (t + 1) + 4 * src + d // 2 + 1))
                    wait(pe, c_free[c], n - 1)
                    for a in range(LT):
                        mm = nc.tensor.transpose(C[c][:, a * P:(a + 1) * P], x_raw[:, c, a * P:(a + 1) * P],
                                                 ident[:, :])
                    mm.then_inc(c_full[c], 1)
                elif kind == "mm":
                    m, a, b = e[1], e[2], e[3]
                    col = D + m * P if m < 4 else (m - 4) * P
                    if a == 0:
                        if isinstance(t, int) and t == -1 and m == 0:
                            pe.wait_ge(w_lo_done, 8)
                        if isinstance(t, int) and t == -1 and m == 4:
                            pe.wait_ge(w_lo_done, 24)
                        wait(pe, c_free[0], use0(t, ("mm", m)) - 1)
                        if m in (0, 4):
                            for c in range(2):
                                pe.wait_ge(c_free[c], use_c(t, c, ("x_turn", m // 4, 6 + c)))
                    for n in range(a, b):
                        d, part = n // 3, n % 3
                        w = (w_lo, w_hi, w_hi)[part]
                        xx = (xT_hi, xT_lo, xT_hi)[part]
                        mm = nc.tensor.matmul(C[0][:, :], w[:, d, col:col + P], xx[:, d, :],
                                              start=(n == 0), stop=(n == 23))
                    if b == 24:
                        mm.then_inc(c_full[0], 1)
                elif kind == "v_turn":
                    j = e[1]
                    n = use1(t, e)
                    wait(pe, c_free[1], n - 1)
                    if j == 0:
                        pe.wait_ge(c_free[0], use0(t - 1, ("mm", 3)))
                    for s in range(ST):
                        mm = nc.tensor.transpose(C[1][:, s * P:(s + 1) * P], vT_sb[:, j, s * P:(s + 1) * P],
                                                 ident[:, :])
                    mm.then_inc(c_full[1], 1)
                elif kind == "mask_turn":
                    st = e[1]
                    n = use1(t, e)
                    wait(pe, c_free[1], n - 1)
                    if st == 0:
                        pe.wait_ge(mask_in, 16 * (t + 2))
                    for a in range(LT):
                        mm = nc.tensor.transpose(C[1][:, a * P:(a + 1) * P], mask_l[:, a, st * P:(st + 1) * P],
                                                 ident[:, :])
                    mm.then_inc(c_full[1], 1)
                elif kind == "shift_turn":
                    G = group(t, g) + 1
                    wait(pe, c_free[1], use1(t, ("shift_turn", g)) - 1)
                    pe.wait_ge(neg_lo, G + 1)
                    nc.tensor.transpose(C[1][0:32, 0:P], shift[:, :].bitcast(F32), ident[:, :])\
                      .then_inc(c_full[1], 1)
                elif kind == "p1":
                    i = e[1]
                    G = group(t, g) + 1
                    b = (g + 1) % 2
                    h, lt = i // 4, i % 4
                    if i == 0:
                        pe.wait_ge(stack_in, 96 * (G + 1))
                    wait(pe, max_done, 16 * G + i - 1)
                    nc.tensor.matmul(S1[i % 2][:, :], q_stack[b][0:96, h, lt * P:(lt + 1) * P], k_stack[b][0:96, :],
                                     start=True, stop=True).then_inc(p1_done, 1)
                elif kind == "p2":
                    i = e[1]
                    G = group(t, g)
                    b = g % 2
                    st, h = i // 4, i % 4
                    if i == 0:
                        pe.wait_ge(shift_in, 32 * (G + 1))
                    wait(pe, exp_done, 16 * G + i - 1)
                    nc.tensor.matmul(S2[i % 2][:, :], k_stack[b][0:98, st * P:(st + 1) * P], q_stack[b][0:98, h, :],
                                     start=True, stop=True).then_inc(p2_done, 1)
                elif kind == "pv":
                    pv(t, group(t, g), g, e[1])
                elif kind == "pv_before" and not (isinstance(t, int) and t == 0 and g == 0):
                    pv(t, group(t, g) - 1, (g - 1) % NG, 3)

            def pv(t, G, g, st):
                pe.wait_ge(exp_done, 16 * G + 4 * st + 4)
                if st == 0:
                    wait(pe, o_out, 2 * G)
                    if g == 0:
                        pe.wait_ge(c_free[1], use1(t, ("v_turn", 1)))
                for h in range(GH):
                    mm = nc.tensor.matmul(O_ps[HD * h:HD * (h + 1), :], v_sb[:, st, HD * g:HD * (g + 1)],
                                          probs[:, 4 * (st % 2) + h, :], start=(st == 0), stop=(st == ST - 1))
                for h in range(GH):
                    mm = nc.tensor.matmul(R_ps[HD * h:HD * (h + 1), :], ones[:, :], probs[:, 4 * (st % 2) + h, :],
                                          start=(st == 0), stop=(st == ST - 1))
                mm.then_inc(pv_done, 1)

            walk(pe, do)
            pv(NB - 1, NB * NG - 1, NG - 1, 3)

            pe.wait_ge(wo_lo_done, 16)

            def batch_rows(b, odd):
                d_hi, d_lo = halves(odd)
                pe.wait_ge(on_lo, NG * (b + 1))
                for lt in range(LT):
                    T = LT * b + lt
                    i = lt % 2
                    for c in range(2):
                        if isinstance(b, int) and b == 0 and lt < 2:
                            pe.wait_ge(exp_done, 16 * NG * NB)
                            pe.wait_ge(max_done, 16 * NG * NB)
                        else:
                            pe.wait_ge(y_added, 2 * (T - 2) + c + 1)
                        for k in range(KD):
                            for n, (o, w) in enumerate(((d_hi, w_lo), (d_lo, w_hi), (d_hi, w_hi))):
                                mm = nc.tensor.matmul(Y[2 * i + c][:, :], o[:, k, lt * P:(lt + 1) * P],
                                                      w[:, k, c * 512:(c + 1) * 512],
                                                      start=(k == 0 and n == 0), stop=(k == KD - 1 and n == 2))
                        mm.then_inc(y_full, 1)

            batch_rows(0, 0)
            batch_rows(1, 1)
            with pe.Fori(1, NB // 2) as p:
                batch_rows(2 * p, 0)
                batch_rows(2 * p + 1, 1)


_INS = ["x", "ctx_2048", "mask_Bx1xSxS2_ff0", "L0_xattn_Wq", "L0_xattn_bq", "L0_xattn_Wk", "L0_xattn_bk",
        "L0_xattn_Wv", "L0_xattn_bv", "L0_xattn_Wo", "L0_xattn_bo", "L0_xattn_gamma", "L0_xattn_beta"]


def kernel(**inputs):
    import numpy as _np
    import concourse.bacc as _bacc
    from concourse import mybir as _mybir
    from concourse.bass_utils import run_bass_kernel_spmd as _run

    nc = _bacc.Bacc("TRN2", target_bir_lowering=False, num_devices=1)
    arrays, args = {}, []
    for name in _INS:
        a = _np.ascontiguousarray(inputs[name])
        arrays[f"in_{name}_dram"] = a
        args.append(nc.dram_tensor(f"in_{name}_dram", a.shape, _mybir.dt.from_np(a.dtype), kind="ExternalInput").ap())
    shape = inputs["x"].shape
    args.append(nc.dram_tensor("out_0_dram", shape, _mybir.dt.float32, kind="ExternalOutput").ap())
    attention_kernel(nc, *args)
    r = _run(nc, [arrays], core_ids=[0])
    return r.results[0]["out_0_dram"]
```

```python
from contextlib import ExitStack

import concourse.bass as bass
from concourse import mybir

F32 = mybir.dt.float32
F32R = mybir.dt.float32r
ALU = mybir.AluOpType
ACT = mybir.ActivationFunctionType

P = 128
LOWEST = -3.4028234e38




HEAD, TAIL = 5, 7
FILL = 8


def timeline(g, project, last):
    at = []

    def put(pos, *entry):
        at.append((pos, len(at), entry))

    more = not (last and g == 7)
    mixed = 32 - HEAD - TAIL
    inner = 16 - HEAD - TAIL
    p2_at = list(range(HEAD)) + [HEAD + (mixed * (n + 1)) // (inner + 1) - 1 for n in range(inner)] + \
        list(range(32 - TAIL, 32))
    p1_at = [pos for pos in range(32) if pos not in p2_at]
    for i, x in enumerate(p2_at):
        put(x, "p2", i)
    if more:
        put(-0.5, "load_stack")
        for i, x in enumerate(p1_at):
            put(x, "p1", i)
        put(p1_at[-1] + 0.4, "shift_neg")
        put(p2_at[-TAIL] + 0.6, "shift_turn")
        put(p2_at[-TAIL + 1] + 0.6, "shift_out")
    put(p2_at[1] + 0.1, "pv_before")
    put(p2_at[2] + 0.1, "out_before")
    put(p2_at[3] + 0.1, "sums_before")
    put(p2_at[7] + 0.1, "sums_out_before")
    for st in range(3):
        put(p2_at[4 * st + 5] + 0.1, "pv", st)
    if g == 0:
        for j in range(2):
            put(1.3 + j, "v_turn", j)
            put(2.2 + j, "v_out", j)
        for st in (2, 3):
            put(6.6 + 2 * (st - 2), "mask_turn", st)
            put(7.6 + 2 * (st - 2), "mask_out", st)
    if g == 7 and more:
        put(-0.7, "load_mask")
        for st in (0, 1):
            put(14.6 + 4 * st, "mask_turn", st)
            put(16.6 + 4 * st, "mask_out", st)
    if project and g in (0, 3):
        src = g // 3
        first = 11.0 if g == 0 else 3.0
        gap = (31.0 - first - 1) / 8
        for d in range(2):
            put(-0.4, "x_load", src, d)
        for d in range(8):
            x = first + gap * d
            put(x, "x_turn", src, d)
            if d + 2 < 8:
                put(x + 0.01, "x_load", src, d + 2)
            put(x + 1.0, "x_hi", src, d)
            put(x + 1.5, "x_lo", src, d)
    if project and g in (1, 2, 4, 5, 6, 7):
        m = 2 * (g - 1) if g < 3 else 4 + 2 * (g - 4)
        where = []
        for pos in range(2, 32):
            alone = pos < HEAD or pos >= 32 - TAIL
            where += [pos + 0.5] * (2 if alone else 1)
        where += [31.8] * FILL
        where = sorted(where + where[HEAD:48])[:48] if len(where) < 48 else where[:24] + where[-24:]
        for n in range(0, 48, 2):
            put(where[n], "mm", m + n // 24, n % 24, n % 24 + 2)
        put(where[23] + 0.7, "keep", m, 0)
        put(where[23] + 1.4, "split", m, 0)
    if g in (2, 3, 5, 6, 7, 0) and (project or g == 0):
        m = {2: 1, 3: 3, 5: 5, 6: 7, 7: 9, 0: 11}[g]
        back = 1 if g == 0 else 0
        put(0.6, "keep", m, back)
        put(1.2, "split", m, back)
    if last and g in (1, 2, 3, 4):
        for n in range(4):
            put(4.5 + 7 * n, "wo_hi_lo", 4 * (g - 1) + n)
    if last and g == 5:
        put(3.5, "recip", 0)
    return [e for _, _, e in sorted(at, key=lambda x: (x[0], x[1]))]


def prologue():
    at = []
    for src in range(2):
        at += [("x_load", src, 0), ("x_load", src, 1)]
        for d in range(8):
            at.append(("x_turn", src, d))
            if d + 2 < 8:
                at.append(("x_load", src, d + 2))
            at += [("x_hi", src, d), ("x_lo", src, d)]
        if src == 0:
            at.append(("load_mask",))
        for m in (range(4) if src == 0 else range(4, 12)):
            at.append(("mm", m, 0, 24))
            at += [("keep", m, 0), ("split", m, 0)]
            if m == 4:
                at.append(("load_stack",))
            if m in (5, 6):
                at += [("mask_turn", m - 5), ("mask_out", m - 5)]
            if m >= 7:
                at += [("p1", i) for i in range(4 * (m - 7), min(4 * (m - 6), 16))]
            if m == 10:
                at += [("shift_neg",), ("shift_turn",), ("shift_out",)]
    return at


def attention_kernel(nc, x, ctx, mask, wq, bq, wk, bk, wv, bv, wo, bo, gamma, beta, out):
    B, L, D = x.shape
    S = ctx.shape[1]
    KV = wk.shape[1]
    HD = 32
    NG = KV // HD
    GH = D // KV
    KD = D // P
    LT, ST = L // P, S // P
    SCALE = float(HD) ** -0.5
    EPS = 1e-6
    NB = B
    assert (L, S, GH * HD, NG, KD) == (512, 512, P, 8, 8)

    STEPS = [timeline(g, True, False) for g in range(NG)]
    LAST = [timeline(g, False, True) for g in range(NG)]
    FIRST = prologue()

    def uses(entries, bank):
        got = []
        for e in entries:
            if e[0] == "x_turn" and e[2] % 2 == bank:
                got.append(e)
            if bank == 0 and e[0] == "mm" and e[2] == 0:
                got.append(("mm", e[1]))
            if bank == 1 and e[0] in ("v_turn", "mask_turn"):
                got.append(e)
        return got

    def spare1(steps):
        got = []
        for g, step in enumerate(steps):
            for e in step:
                if e[0] == "shift_turn":
                    got.append(("shift_turn", g))
                else:
                    got += uses([e], 1)
        return got

    BODY0 = [u for step in STEPS for u in uses(step, 0)]
    FIRST0 = uses(FIRST, 0)
    BODY1, LAST1 = spare1(STEPS), spare1(LAST)
    FIRST1 = [("shift_turn", NG - 1) if e[0] == "shift_turn" else e
              for e in FIRST if e[0] == "shift_turn" or uses([e], 1)]
    assert len(BODY0) == len(FIRST0) == 20

    def use0(t, key):
        return FIRST0.index(key) + 1 if isinstance(t, int) and t < 0 else 20 * (t + 1) + BODY0.index(key) + 1

    def use1(t, key):
        if isinstance(t, int) and t < 0:
            return FIRST1.index(key) + 1
        order = LAST1 if isinstance(t, int) and t == NB - 1 else BODY1
        return len(FIRST1) + len(BODY1) * t + order.index(key) + 1

    with ExitStack() as stack:
        def sb(name, shape, dt, where=stack):
            return where.enter_context(nc.sbuf_tensor(name, shape, dt))

        def sem(name):
            return stack.enter_context(nc.semaphore(name))

        def dram(name, shape, dt):
            return nc.dram_tensor(name, shape, dt, kind="Internal").ap()

        q_hi_d = dram("q_hi_d", [NB * NG, P, L], F32)
        q_lo_d = dram("q_lo_d", [NB * NG, P, L], F32)
        k_hi_d = dram("k_hi_d", [NB * 2, P, S], F32)
        k_lo_d = dram("k_lo_d", [NB * 2, P, S], F32)
        o_d = dram("o_d", [NB * NG, P, L], F32)
        r_d = dram("r_d", [NB * NG, GH, L], F32)
        ri_d = dram("ri_d", [NB * NG, GH, L], F32)

        w_hi = sb("w_hi", [P, KD, D + 2 * KV], F32R)
        w_lo = sb("w_lo", [P, KD, D + 2 * KV], F32R)
        xT_hi = sb("xT_hi", [P, KD, L], F32R)
        xT_lo = sb("xT_lo", [P, KD, L], F32R)
        x_raw = sb("x_raw", [P, 2, L], F32)
        ident = sb("ident", [P, P], F32)
        ones = sb("ones", [P, HD], F32)
        bq_c = sb("bq_c", [P, NG], F32)
        bq_s = sb("bq_s", [P, NG], F32)
        bkv_c = sb("bkv_c", [P, 4], F32)
        eps_c = sb("eps_c", [P, 1], F32)
        row_max = sb("row_max", [P, 4 * GH], F32)
        shift = sb("shift", [P, 2 * 4 * GH], F32R)
        shift_rows = sb("shift_rows", [2 * 4 * GH, P], F32R)
        vT_sb = sb("vT_sb", [P, 2, S], F32)
        sums = vT_sb[:, :, :].rearrange("p a s -> p (a s)")
        assert NG * NB * GH * L // P == 2 * S
        EARLY = NG * (NB - 1) * GH * L // P
        with ExitStack() as first_part:
            def sb1(name, shape, dt):
                return sb(name, shape, dt, first_part)

            mask_l = sb1("mask_l", [P, LT, S], F32)
            mask_s = sb1("mask_s", [P, ST, L], F32)
            probs = sb1("probs", [P, 8, L], F32)
            q_stack = [sb1(f"q_stack{i}", [98, GH, L], F32R) for i in range(2)]
            k_stack = [sb1(f"k_stack{i}", [98, S], F32R) for i in range(2)]
            v_sb = sb1("v_sb", [P, ST, KV], F32)
            part = sb1("part", [P, L], F32)
            part_hi = sb1("part_hi", [P, L], F32R)
            acc = sb1("acc", [P, GH, L], F32)
            out_sb = sb1("out_sb", [P, L], F32)
        o_raw = sb("o_raw", [P, 4, L], F32)
        r_inv = sb("r_inv", [P, 4, L], F32)
        x_res = sb("x_res", [P, 2, D], F32)
        y_sb = sb("y_sb", [P, 2, D], F32)
        z_sb = sb("z_sb", [P, 2, D], F32)
        bo_b = sb("bo_b", [P, D], F32)
        gamma_b = sb("gamma_b", [P, D], F32)
        beta_b = sb("beta_b", [P, D], F32)
        stats = sb("stats", [P, 2, 6], F32)
        mean_var = sb("mean_var", [P, 2], F32)
        std = sb("std", [P, 1], F32)
        rstd = sb("rstd", [P, 1], F32)

        bank = [stack.enter_context(nc.psum_tensor(f"bank{i}", [P, 512], F32)) for i in range(8)]
        S1, S2, O_ps, R_ps, C = bank[0:2], bank[2:4], bank[4], bank[5], bank[6:8]
        Y = bank[0:4]

        consts_ready = sem("consts_ready")
        biases_in = sem("biases_in")
        bias_scaled = sem("bias_scaled")
        w_in = [sem(f"w_in{i}") for i in range(8)]
        w_hi_done, w_lo_done = sem("w_hi_done"), sem("w_lo_done")
        x_in = [sem("x_in0"), sem("x_in1")]
        c_full = [sem("c_full0"), sem("c_full1")]
        c_free = [sem("c_free0"), sem("c_free1")]
        x_hi_done = sem("x_hi_done")
        part_hi_done, part_lo_done = sem("part_hi_done"), sem("part_lo_done")
        qk_stored = sem("qk_stored")
        mask_in = sem("mask_in")
        stack_in = sem("stack_in")
        p1_done, max_done = sem("p1_done"), sem("max_done")
        neg_hi, neg_lo = sem("neg_hi"), sem("neg_lo")
        shift_in = sem("shift_in")
        p2_done, masked, exp_done = sem("p2_done"), sem("masked"), sem("exp_done")
        pv_done = sem("pv_done")
        acc_done, sum_done = sem("acc_done"), sem("sum_done")
        o_out, r_out, out_stored = sem("o_out"), sem("r_out"), sem("out_stored")
        wo_in = [sem("wo_in0"), sem("wo_in1")]
        wo_hi_done, wo_lo_done = sem("wo_hi_done"), sem("wo_lo_done")
        r_in, r_done, ri_stored = sem("r_in"), sem("r_done"), sem("ri_stored")
        rows_in = sem("rows_in")
        o_in = [sem(f"o_in{i}") for i in range(4)]
        normed, on_hi, on_lo = sem("normed"), sem("on_hi"), sem("on_lo")
        res_in = [sem("res_in0"), sem("res_in1")]
        res_bo = sem("res_bo")
        y_full, y_added = sem("y_full"), sem("y_added")
        y_stat, y_mv, y_std, y_rstd, y_cen = (sem(n) for n in ("y_stat", "y_mv", "y_std", "y_rstd", "y_cen"))
        z_done = sem("z_done")
        z_stored = [sem("z_stored0"), sem("z_stored1")]

        SPLITS = [0, 1, 4, 5, 6, 7, 8, 9, 10, 11]

        def x_hi_no(t, src, d):
            return 2 * KD * (t + 1) + KD * src + d + 1

        def split_no(t, m):
            return 10 * (t + 1) + SPLITS.index(m) + 1

        def wait(eng, s, value):
            if not (isinstance(value, int) and value <= 0):
                eng.wait_ge(s, value)

        def counted_ahead(eng, *values):
            for v in values:
                if not isinstance(v, int):
                    eng.lower_val(v)

        def walk(eng, do):
            for e in FIRST:
                do(-1, NG - 1, e)
            for g in range(NG):
                for e in STEPS[g]:
                    do(0, g, e)
            with eng.Fori(1, NB - 1) as t:
                for g in range(NG):
                    for e in STEPS[g]:
                        do(t, g, e)
            for g in range(NG):
                for e in LAST[g]:
                    do(NB - 1, g, e)

        def group(t, g):
            return NG * t + g

        def first(t, g):
            return isinstance(t, int) and t == 0 and g == 0

        def made_before(t, e):
            return isinstance(t, int) and t == 0 and e[2] == 1

        def use_c(t, c, key):
            return use0(t, key) if c == 0 else use1(t, key)

        def use_of_turn(t, src, d):
            if d >= 2:
                return use_c(t, d % 2, ("x_turn", src, d - 2))
            if src == 1:
                return use_c(t, d % 2, ("x_turn", 0, d + 6))
            if isinstance(t, int) and t < 0:
                return 0
            return use_c(t - 1, d % 2, ("x_turn", 1, d + 6))

        def mask_use(t, st):
            if st < 2:
                return use1(t - 1, ("mask_turn", st))
            return use1(t, ("mask_turn", st))

        def w_place(n):
            return (n // 2, (n % 2) * 512) if n < 16 else (n - 16, D)

        def rows_of(a, part):
            cut = NG * (NB - 1)
            r = (a[0:cut] if part == 0 else a[cut:NG * NB]).rearrange("g h l -> (g h l)")
            return r.rearrange("(p f) -> p f", p=P)

        def halves(odd):
            if odd:
                return w_hi[:, :, D:D + 512], w_lo[:, :, D:D + 512]
            return xT_hi[:, :, :], xT_lo[:, :, :]

        block = stack.enter_context(nc.Block())

        @block.sync
        def _(sp):
            def w_piece(n):
                if n < 16:
                    return [(slice(0, 512), wq[(n // 2) * P:(n // 2 + 1) * P, (n % 2) * 512:(n % 2 + 1) * 512])]
                k = n - 16
                return [(slice(0, KV), wk[k * P:(k + 1) * P, :]), (slice(KV, 2 * KV), wv[k * P:(k + 1) * P, :])]

            order = list(range(16, 24)) + list(range(16))
            for k, n in enumerate(order):
                if k >= 8:
                    sp.wait_ge(w_lo_done, k - 7)
                for cols, src in w_piece(n):
                    sp.dma_start(probs[:, k % 8, cols], src).then_inc(w_in[k % 8], 16)
                if k == 0:
                    with nc.allow_non_contiguous_dma(reason="bias columns, once"):
                        sp.dma_start(bq_c[:, :], bq.rearrange("(g p) -> p g", p=P)).then_inc(biases_in, 16)
                        sp.dma_start(bkv_c[:, 0:2], bk.rearrange("(g p) -> p g", p=P)).then_inc(biases_in, 16)
                        sp.dma_start(bkv_c[:, 2:4], bv.rearrange("(g p) -> p g", p=P)).then_inc(biases_in, 16)

            def do(t, g, e):
                kind = e[0]
                if kind == "x_load":
                    src, d = e[1], e[2]
                    before = use_of_turn(t, src, d)
                    wait(sp, c_full[d % 2], before)
                    dram_in = (ctx, x)[src][t + 1].rearrange("(a p) d -> p a d", p=P)[:, :, d * P:(d + 1) * P]
                    sp.dma_start(x_raw[:, d % 2, :].rearrange("p (a d) -> p a d", a=LT), dram_in)\
                      .then_inc(x_in[d % 2], 16)
                elif kind == "load_mask":
                    wait(sp, max_done, 128 * (t + 1))
                    sp.dma_start(mask_l[:, :, :], mask[t + 1, 0].rearrange("(a p) s -> p a s", p=P))\
                      .then_inc(mask_in, 16)
                elif kind == "split" and e[1] not in (2, 3) and not made_before(t, e):
                    m, nt = e[1], t - e[2]
                    sp.wait_ge(part_lo_done, split_no(nt, m))
                    hi_dst, lo_dst = (k_hi_d, k_lo_d) if m < 2 else (q_hi_d, q_lo_d)
                    row = 2 * (nt + 1) + m if m < 2 else NG * (nt + 1) + m - 4
                    sp.dma_start(hi_dst[row], part_hi[:, :].bitcast(F32)).then_inc(qk_stored, 16)
                    sp.dma_start(lo_dst[row], part[:, :]).then_inc(qk_stored, 16)
                elif kind == "load_stack":
                    G = group(t, g) + 1
                    b = (g + 1) % 2
                    nt, ng = (t, g + 1) if g + 1 < NG else (t + 1, 0)
                    counts = 16 * (G - 1), 32 * split_no(nt - 1, 4 + ng)
                    counted_ahead(sp, *counts)
                    wait(sp, p2_done, counts[0])
                    wait(sp, qk_stored, counts[1])
                    q_hi, q_lo = (a[G].rearrange("(h d) l -> d h l", h=GH) for a in (q_hi_d, q_lo_d))
                    kr = 2 * nt + ng // 4
                    k0 = HD * (ng % 4)
                    k_hi, k_lo = (a[kr][k0:k0 + HD, :] for a in (k_hi_d, k_lo_d))
                    for i, (q, k) in enumerate(((q_hi, k_hi), (q_lo, k_hi), (q_hi, k_lo))):
                        sp.dma_start(k_stack[b][HD * i:HD * (i + 1), :].bitcast(F32), k).then_inc(stack_in, 16)
                        sp.dma_start(q_stack[b][HD * i:HD * (i + 1), :, :].bitcast(F32), q).then_inc(stack_in, 16)
                elif kind == "shift_out":
                    G = group(t, g) + 1
                    b = (g + 1) % 2
                    wait(sp, c_free[1], use1(t, ("shift_turn", g)))
                    for r in range(2):
                        sp.dma_start(q_stack[b][96 + r:97 + r, :, :].bitcast(F32),
                                     shift_rows[16 * r:16 * (r + 1), :].bitcast(F32)).then_inc(shift_in, 16)
                elif kind == "out_before" and not first(t, g):
                    store_o(group(t, g) - 1)
                elif kind == "sums_out_before" and not first(t, g):
                    store_r(group(t, g) - 1)
                elif kind == "wo_hi_lo":
                    n = e[1]
                    if n >= 2:
                        sp.wait_ge(wo_lo_done, n - 1)
                    sp.dma_start(x_raw[:, n % 2, :], wo[(n // 2) * P:(n // 2 + 1) * P,
                                                        (n % 2) * 512:(n % 2 + 1) * 512]).then_inc(wo_in[n % 2], 16)
                elif kind == "recip":
                    sp.wait_ge(out_stored, 32 * NG * (NB - 1))
                    sp.dma_start(sums[:, 0:EARLY], rows_of(r_d, 0)).then_inc(r_in, 16)
                    sp.wait_ge(r_done, 1)
                    sp.dma_start(rows_of(ri_d, 0), sums[:, 0:EARLY]).then_inc(ri_stored, 16)

            def store_o(G):
                sp.wait_ge(o_out, G + 1)
                sp.dma_start(o_d[G], out_sb[:, :]).then_inc(out_stored, 16)

            def store_r(G):
                sp.wait_ge(r_out, G + 1)
                sp.dma_start(r_d[G], out_sb[0:P:HD, :]).then_inc(out_stored, 16)

            walk(sp, do)
            store_o(NB * NG - 1)
            store_r(NB * NG - 1)

            sp.wait_ge(out_stored, 32 * NG * NB)
            sp.dma_start(sums[:, EARLY:], rows_of(r_d, 1)).then_inc(r_in, 16)
            sp.dma_start(bo_b[:, :], bo.rearrange("(a d) -> a d", a=1).broadcast_to([P, D])).then_inc(rows_in, 16)
            sp.dma_start(gamma_b[:, :], gamma.rearrange("(a d) -> a d", a=1).broadcast_to([P, D])).then_inc(rows_in, 16)
            sp.dma_start(beta_b[:, :], beta.rearrange("(a d) -> a d", a=1).broadcast_to([P, D])).then_inc(rows_in, 16)

            def load_o(b, g):
                n = NG * b + g
                wait(sp, on_lo, n - 3)
                sp.dma_start(o_raw[:, g % 4, :], o_d[n]).then_inc(o_in[g % 4], 16)
                for h in range(GH):
                    sp.dma_start(r_inv[HD * h:HD * (h + 1), g % 4, :],
                                 ri_d[n][h:h + 1, :].broadcast_to([HD, L])).then_inc(o_in[g % 4], 16)

            def load_res(b, lt):
                T = LT * b + lt
                wait(sp, y_added, 2 * (T - 1))
                sp.dma_start(x_res[:, lt % 2, :], x[b, lt * P:(lt + 1) * P, :]).then_inc(res_in[lt % 2], 16)

            def store(b, lt):
                T = LT * b + lt
                sp.wait_ge(z_done, T + 1)
                sp.dma_start(out[b, lt * P:(lt + 1) * P, :], z_sb[:, lt % 2, :]).then_inc(z_stored[lt % 2], 16)

            sp.wait_ge(ri_stored, 16)
            for g in range(NG):
                load_o(0, g)
                if g == 3:
                    load_res(0, 0)
                    load_res(0, 1)
            sp.wait_ge(r_done, 2)
            sp.dma_start(rows_of(ri_d, 1), sums[:, EARLY:]).then_inc(ri_stored, 16)
            sp.wait_ge(ri_stored, 32)
            load_o(1, 0)
            load_o(1, 1)

            def batch_rows(b, more, further):
                for lt in range(LT):
                    if lt < 3 and more:
                        load_o(b + 1, 2 * lt + 2)
                        load_o(b + 1, 2 * lt + 3)
                    if lt == 3 and further:
                        load_o(b + 2, 0)
                        load_o(b + 2, 1)
                    store(b, lt)
                    if lt >= 2 and more:
                        load_res(b + 1, lt - 2)
                    elif lt < 2:
                        load_res(b, lt + 2)

            batch_rows(0, True, True)
            with sp.Fori(1, NB - 2) as b:
                batch_rows(b, True, True)
            batch_rows(NB - 2, True, False)
            batch_rows(NB - 1, False, False)
            sp.wait_ge(z_stored[0], 16 * 2 * NB)
            sp.wait_ge(z_stored[1], 16 * 2 * NB)

        @block.gpsimd
        def _(pool):
            nc.gpsimd.memset(ident[:, :], 0.0).then_inc(consts_ready, 1)
            nc.gpsimd.memset(ones[:, :], 1.0).then_inc(consts_ready, 1)
            nc.gpsimd.memset(eps_c[:, :], EPS).then_inc(consts_ready, 1)
            for i in range(2):
                pool.wait_ge(consts_ready, 3 + i)
                nc.gpsimd.memset(k_stack[i][96:98, :].bitcast(F32), 1.0).then_inc(consts_ready, 1)
            pool.wait_ge(consts_ready, 5)
            nc.gpsimd.affine_select(out=ident[:, :], in_=ident[:, :], compare_op=ALU.not_equal, fill=1.0, base=0,
                                    pattern=[[-1, P]], channel_multiplier=1).then_inc(consts_ready, 1)

            def do(t, g, e):
                kind = e[0]
                if kind == "split" and e[1] not in (2, 3) and not made_before(t, e):
                    pool.wait_ge(part_hi_done, split_no(t - e[2], e[1]))
                    nc.gpsimd.tensor_tensor(part[:, :], part[:, :], part_hi[:, :].bitcast(F32), ALU.subtract)\
                      .then_inc(part_lo_done, 1)
                elif kind == "p2" and e[1] >= 4:
                    i = e[1]
                    G = group(t, g)
                    st, h = i // 4, i % 4
                    if st == 1 and h == 0:
                        wait(pool, sum_done, G)
                    if st >= 2:
                        pool.wait_ge(acc_done, 12 * G + 4 * (st - 2) + h + 1)
                    pool.wait_ge(exp_done, 16 * G + i + 1)
                    nc.gpsimd.tensor_tensor(acc[:, h, :], probs[:, h, :] if st == 1 else acc[:, h, :],
                                            probs[:, 4 * (st % 2) + h, :], ALU.add).then_inc(acc_done, 1)

                elif kind == "wo_hi_lo":
                    n = e[1]
                    pool.wait_ge(wo_hi_done, n + 1)
                    k, c = n // 2, (n % 2) * 512
                    nc.gpsimd.tensor_tensor(w_lo[:, k, c:c + 512], x_raw[:, n % 2, :],
                                            w_hi[:, k, c:c + 512].bitcast(F32), ALU.subtract).then_inc(wo_lo_done, 1)

            walk(pool, do)

            def lo(b, g, odd):
                n = NG * b + g
                _, d_lo = halves(odd)
                d_hi, _ = halves(odd)
                pool.wait_ge(on_hi, n + 1)
                nc.gpsimd.tensor_tensor(d_lo[:, g, :], o_raw[:, g % 4, :], d_hi[:, g, :].bitcast(F32),
                                        ALU.subtract).then_inc(on_lo, 1)

            def residual(b, lt):
                T = LT * b + lt
                pool.wait_ge(res_in[lt % 2], 16 * (2 * b + lt // 2 + 1))
                nc.gpsimd.tensor_tensor(x_res[:, lt % 2, :], x_res[:, lt % 2, :], bo_b[:, :], ALU.add)\
                  .then_inc(res_bo, 1)

            for g in range(NG):
                lo(0, g, 0)
            pool.wait_ge(rows_in, 48)

            def batch_rows(b, odd, more):
                for lt in range(LT):
                    residual(b, lt)
                    if more:
                        lo(b + 1, 2 * lt, 1 - odd)
                        lo(b + 1, 2 * lt + 1, 1 - odd)

            with pool.Fori(0, NB // 2 - 1) as p:
                batch_rows(2 * p, 0, True)
                batch_rows(2 * p + 1, 1, True)
            batch_rows(NB - 2, 0, True)
            batch_rows(NB - 1, 1, False)

        @block.scalar
        def _(act):
            order = list(range(16, 24)) + list(range(16))
            count = [0] * 8
            for k, n in enumerate(order):
                count[k % 8] += 32 if n >= 16 else 16
                act.wait_ge(w_in[k % 8], count[k % 8])
                d, c = w_place(n)
                nc.scalar.activation(w_hi[:, d, c:c + 512], probs[:, k % 8, :], ACT.Copy).then_inc(w_hi_done, 1)
            act.wait_ge(biases_in, 48)
            nc.scalar.mul(bq_s[:, :], bq_c[:, :], SCALE).then_inc(bias_scaled, 1)
            act.wait_ge(bias_scaled, 1)

            def do(t, g, e):
                kind = e[0]
                if kind == "x_hi":
                    src, d = e[1], e[2]
                    act.wait_ge(c_full[d % 2], use_c(t, d % 2, ("x_turn", src, d)))
                    nc.scalar.activation(xT_hi[:, d, :], C[d % 2][:, :], ACT.Copy).then_inc(x_hi_done, 1)
                elif kind == "keep" and not made_before(t, e):
                    m, nt = e[1], t - e[2]
                    act.wait_ge(c_full[0], use0(nt, ("mm", m)))
                    if m in (2, 3):
                        nc.scalar.activation(vT_sb[:, m - 2, :], C[0][:, :], ACT.Identity, bias=bkv_c[:, m:m + 1])\
                          .then_inc(c_free[0], 1)
                    else:
                        wait(act, qk_stored, 32 * (split_no(nt, m) - 1))
                        scale, bias = (1.0, bkv_c[:, m:m + 1]) if m < 2 else (SCALE, bq_s[:, m - 4:m - 3])
                        nc.scalar.activation(part[:, :], C[0][:, :], ACT.Identity, scale=scale, bias=bias)\
                          .then_inc(c_free[0], 1)
                elif kind == "split" and e[1] not in (2, 3) and not made_before(t, e):
                    act.wait_ge(c_free[0], use0(t - e[2], ("mm", e[1])))
                    nc.scalar.activation(part_hi[:, :], part[:, :], ACT.Copy).then_inc(part_hi_done, 1)
                elif kind == "v_out":
                    j = e[1]
                    act.wait_ge(c_full[1], use1(t, ("v_turn", j)))
                    wait(act, pv_done, 4 * NG * t)
                    nc.scalar.activation(v_sb[:, :, j * P:(j + 1) * P],
                                         C[1][:, :].rearrange("p (s d) -> p s d", s=ST), ACT.Copy)\
                      .then_inc(c_free[1], 1)
                elif kind == "mask_out":
                    st = e[1]
                    act.wait_ge(c_full[1], use1(t, ("mask_turn", st)))
                    nt = t + 1 if g == 7 else t
                    wait(act, masked, 128 * nt - 16 + 4 * st + 4 if not (isinstance(nt, int) and nt == 0) else 0)
                    nc.scalar.activation(mask_s[:, st, :], C[1][:, :], ACT.Copy).then_inc(c_free[1], 1)
                elif kind == "shift_out":
                    G = group(t, g) + 1
                    act.wait_ge(c_full[1], use1(t, ("shift_turn", g)))
                    wait(act, shift_in, 32 * G)
                    nc.scalar.activation(shift_rows[:, :], C[1][0:32, 0:P], ACT.Copy).then_inc(c_free[1], 1)
                elif kind == "p2":
                    i = e[1]
                    n = 16 * group(t, g) + i
                    act.wait_ge(masked, n + 1)
                    wait(act, pv_done, 4 * group(t, g) + i // 4 - 1)
                    st, h = i // 4, i % 4
                    wait(act, acc_done, 12 * group(t, g) + (h - 7, h - 3, h + 1, h + 1)[st])
                    nc.scalar.activation(probs[:, i % 8, :], S2[i % 2][:, :], ACT.Exp).then_inc(exp_done, 1)
                elif kind == "out_before" and not first(t, g):
                    out_o(group(t, g) - 1)
                elif kind == "sums_out_before" and not first(t, g):
                    out_r(group(t, g) - 1)
                elif kind == "wo_hi_lo":
                    n = e[1]
                    act.wait_ge(wo_in[n % 2], 16 * (n // 2 + 1))
                    k, c = n // 2, (n % 2) * 512
                    act.wait_ge(c_full[0], 20 * NB)
                    nc.scalar.activation(w_hi[:, k, c:c + 512], x_raw[:, n % 2, :], ACT.Copy).then_inc(wo_hi_done, 1)

            def out_o(G):
                act.wait_ge(pv_done, 4 * (G + 1))
                wait(act, out_stored, 32 * G)
                nc.scalar.activation(out_sb[:, :], O_ps[:, :], ACT.Copy).then_inc(o_out, 1)

            def out_r(G):
                act.wait_ge(sum_done, G + 1)
                act.wait_ge(out_stored, 32 * G + 16)
                nc.scalar.activation(out_sb[:, :], R_ps[:, :], ACT.Copy).then_inc(r_out, 1)

            walk(act, do)
            out_o(NB * NG - 1)
            out_r(NB * NG - 1)

            def hi(b, g, odd):
                n = NG * b + g
                d_hi, _ = halves(odd)
                act.wait_ge(normed, n + 1)
                wait(act, y_full, 8 * (b - 1) if not (isinstance(b, int) and b == 0) else 0)
                nc.scalar.activation(d_hi[:, g, :], o_raw[:, g % 4, :], ACT.Copy).then_inc(on_hi, 1)

            def root(b, lt):
                T = LT * b + lt
                act.wait_ge(y_mv, T + 1)
                nc.scalar.activation(std[:, :], mean_var[:, 1:2], ACT.Sqrt, bias=eps_c[:, :]).then_inc(y_std, 1)

            for g in range(NG):
                hi(0, g, 0)

            def batch_rows(b, odd, more):
                for lt in range(LT):
                    if more:
                        hi(b + 1, 2 * lt, 1 - odd)
                        hi(b + 1, 2 * lt + 1, 1 - odd)
                    root(b, lt)

            batch_rows(0, 0, True)
            batch_rows(1, 1, True)
            with act.Fori(1, NB // 2 - 1) as p:
                batch_rows(2 * p, 0, True)
                batch_rows(2 * p + 1, 1, True)
            batch_rows(NB - 2, 0, True)
            batch_rows(NB - 1, 1, False)

        @block.vector
        def _(dve):
            order = list(range(16, 24)) + list(range(16))
            for k, n in enumerate(order):
                dve.wait_ge(w_hi_done, k + 1)
                d, c = w_place(n)
                nc.vector.tensor_tensor(w_lo[:, d, c:c + 512], probs[:, k % 8, :],
                                        w_hi[:, d, c:c + 512].bitcast(F32), ALU.subtract).then_inc(w_lo_done, 1)

            def do(t, g, e):
                kind = e[0]
                if kind == "x_lo":
                    src, d = e[1], e[2]
                    dve.wait_ge(x_hi_done, x_hi_no(t, src, d))
                    nc.vector.tensor_tensor(xT_lo[:, d, :], C[d % 2][:, :], xT_hi[:, d, :].bitcast(F32),
                                            ALU.subtract).then_inc(c_free[d % 2], 1)
                elif kind == "p1":
                    i = e[1]
                    n = 16 * (group(t, g) + 1) + i
                    h, lt = i // 4, i % 4
                    if i == 0:
                        dve.wait_ge(mask_in, 16 * (t + 2) if g == 7 else 16 * (t + 1))
                    counted_ahead(dve, n + 1)
                    dve.wait_ge(w_hi_done, 24)
                    dve.wait_ge(p1_done, n + 1)
                    nc.vector.tensor_tensor_reduce(out=S1[i % 2][:, :], in0=S1[i % 2][:, :], in1=mask_l[:, lt, :],
                                                   scale=1.0, scalar=LOWEST, op0=ALU.add, op1=ALU.max,
                                                   accum_out=row_max[:, i:i + 1]).then_inc(max_done, 1)
                elif kind == "shift_neg":
                    G = group(t, g) + 1
                    dve.wait_ge(max_done, 16 * (G + 1))
                    if not (isinstance(t, int) and t < 0):
                        pt, pg = (t, g - 1) if g > 0 else (t - 1, NG - 1)
                        dve.wait_ge(c_full[1], use1(pt, ("shift_turn", pg)))
                    nc.vector.tensor_scalar(shift[:, 0:16], row_max[:, :], -1.0, None, ALU.mult).then_inc(neg_hi, 1)
                    dve.wait_ge(neg_hi, G + 1)
                    nc.vector.scalar_tensor_tensor(out=shift[:, 16:32], in0=row_max[:, :], scalar=-1.0,
                                                   in1=shift[:, 0:16].bitcast(F32), op0=ALU.mult, op1=ALU.subtract)\
                      .then_inc(neg_lo, 1)
                elif kind == "p2":
                    i = e[1]
                    st = i // 4
                    n = 16 * group(t, g) + i
                    if g == 0 and i % 4 == 0:
                        dve.wait_ge(c_free[1], mask_use(t, st))
                    dve.wait_ge(p2_done, n + 1)
                    nc.vector.tensor_tensor(S2[i % 2][:, :], S2[i % 2][:, :], mask_s[:, st, :], ALU.add)\
                      .then_inc(masked, 1)
                elif kind == "recip":
                    dve.wait_ge(r_in, 16)
                    nc.vector.reciprocal(sums[:, 0:EARLY], sums[:, 0:EARLY]).then_inc(r_done, 1)

            walk(dve, do)
            dve.wait_ge(r_in, 32)
            nc.vector.reciprocal(sums[:, EARLY:], sums[:, EARLY:]).then_inc(r_done, 1)

            def norm(b, g):
                n = NG * b + g
                dve.wait_ge(o_in[g % 4], 80 * (2 * b + g // 4 + 1))
                nc.vector.tensor_tensor(o_raw[:, g % 4, :], o_raw[:, g % 4, :], r_inv[:, g % 4, :], ALU.mult)\
                  .then_inc(normed, 1)

            for g in range(NG):
                norm(0, g)

            def rows(b, lt):
                T = LT * b + lt
                i = lt % 2
                dve.wait_ge(res_bo, T + 1)
                for c in range(2):
                    dve.wait_ge(y_full, 2 * T + c + 1)
                    nc.vector.tensor_tensor(y_sb[:, i, c * 512:(c + 1) * 512], Y[2 * i + c][:, :],
                                            x_res[:, i, c * 512:(c + 1) * 512], ALU.add).then_inc(y_added, 1)
                for c in range(2):
                    dve.wait_ge(y_added, 2 * T + c + 1)
                    nc.vector.bn_stats(stats[:, c, :], y_sb[:, i, c * 512:(c + 1) * 512]).then_inc(y_stat, 1)
                dve.wait_ge(wo_hi_done, 16)
                dve.wait_ge(y_stat, 2 * T + 2)
                nc.vector.bn_aggr(mean_var[:, :], stats[:, :, :]).then_inc(y_mv, 1)
                dve.wait_ge(y_mv, T + 1)
                wait(dve, z_stored[i], 16 * (2 * b + lt // 2))
                nc.vector.scalar_tensor_tensor(out=z_sb[:, i, :], in0=y_sb[:, i, :], scalar=mean_var[:, 0:1],
                                               in1=gamma_b[:, :], op0=ALU.subtract, op1=ALU.mult).then_inc(y_cen, 1)
                dve.wait_ge(y_std, T + 1)
                nc.vector.reciprocal(rstd[:, :], std[:, :]).then_inc(y_rstd, 1)
                dve.wait_ge(y_rstd, T + 1)
                dve.wait_ge(y_cen, T + 1)
                nc.vector.scalar_tensor_tensor(out=z_sb[:, i, :], in0=z_sb[:, i, :], scalar=rstd[:, :],
                                               in1=beta_b[:, :], op0=ALU.mult, op1=ALU.add).then_inc(z_done, 1)

            def batch_rows(b, more):
                for lt in range(LT):
                    if more:
                        norm(b + 1, 2 * lt)
                        norm(b + 1, 2 * lt + 1)
                    rows(b, lt)

            batch_rows(0, True)
            with dve.Fori(1, NB - 1) as b:
                batch_rows(b, True)
            batch_rows(NB - 1, False)

        @block.tensor
        def _(pe):
            pe.wait_ge(consts_ready, 6)

            def do(t, g, e):
                kind = e[0]
                if kind == "x_turn":
                    src, d = e[1], e[2]
                    c = d % 2
                    n = use_c(t, c, ("x_turn", src, d))
                    pe.wait_ge(x_in[c], 16 * (8 * (t + 1) + 4 * src + d // 2 + 1))
                    wait(pe, c_free[c], n - 1)
                    for a in range(LT):
                        mm = nc.tensor.transpose(C[c][:, a * P:(a + 1) * P], x_raw[:, c, a * P:(a + 1) * P],
                                                 ident[:, :])
                    mm.then_inc(c_full[c], 1)
                elif kind == "mm":
                    m, a, b = e[1], e[2], e[3]
                    col = D + m * P if m < 4 else (m - 4) * P
                    if a == 0:
                        if isinstance(t, int) and t == -1 and m == 0:
                            pe.wait_ge(w_lo_done, 8)
                        if isinstance(t, int) and t == -1 and m == 4:
                            pe.wait_ge(w_lo_done, 24)
                        wait(pe, c_free[0], use0(t, ("mm", m)) - 1)
                        if m in (0, 4):
                            for c in range(2):
                                pe.wait_ge(c_free[c], use_c(t, c, ("x_turn", m // 4, 6 + c)))
                    for n in range(a, b):
                        d, part = n // 3, n % 3
                        w = (w_lo, w_hi, w_hi)[part]
                        xx = (xT_hi, xT_lo, xT_hi)[part]
                        mm = nc.tensor.matmul(C[0][:, :], w[:, d, col:col + P], xx[:, d, :],
                                              start=(n == 0), stop=(n == 23))
                    if b == 24:
                        mm.then_inc(c_full[0], 1)
                elif kind == "v_turn":
                    j = e[1]
                    n = use1(t, e)
                    wait(pe, c_free[1], n - 1)
                    if j == 0:
                        pe.wait_ge(c_free[0], use0(t - 1, ("mm", 3)))
                    for s in range(ST):
                        mm = nc.tensor.transpose(C[1][:, s * P:(s + 1) * P], vT_sb[:, j, s * P:(s + 1) * P],
                                                 ident[:, :])
                    mm.then_inc(c_full[1], 1)
                elif kind == "mask_turn":
                    st = e[1]
                    n = use1(t, e)
                    wait(pe, c_free[1], n - 1)
                    if st == 0:
                        pe.wait_ge(mask_in, 16 * (t + 2))
                    for a in range(LT):
                        mm = nc.tensor.transpose(C[1][:, a * P:(a + 1) * P], mask_l[:, a, st * P:(st + 1) * P],
                                                 ident[:, :])
                    mm.then_inc(c_full[1], 1)
                elif kind == "shift_turn":
                    G = group(t, g) + 1
                    wait(pe, c_free[1], use1(t, ("shift_turn", g)) - 1)
                    pe.wait_ge(neg_lo, G + 1)
                    nc.tensor.transpose(C[1][0:32, 0:P], shift[:, :].bitcast(F32), ident[:, :])\
                      .then_inc(c_full[1], 1)
                elif kind == "p1":
                    i = e[1]
                    G = group(t, g) + 1
                    b = (g + 1) % 2
                    h, lt = i // 4, i % 4
                    if i == 0:
                        pe.wait_ge(stack_in, 96 * (G + 1))
                    wait(pe, max_done, 16 * G + i - 1)
                    nc.tensor.matmul(S1[i % 2][:, :], q_stack[b][0:96, h, lt * P:(lt + 1) * P], k_stack[b][0:96, :],
                                     start=True, stop=True).then_inc(p1_done, 1)
                elif kind == "p2":
                    i = e[1]
                    G = group(t, g)
                    b = g % 2
                    st, h = i // 4, i % 4
                    if i == 0:
                        pe.wait_ge(shift_in, 32 * (G + 1))
                    wait(pe, exp_done, 16 * G + i - 1)
                    nc.tensor.matmul(S2[i % 2][:, :], k_stack[b][0:98, st * P:(st + 1) * P], q_stack[b][0:98, h, :],
                                     start=True, stop=True).then_inc(p2_done, 1)
                elif kind == "pv":
                    pv(t, group(t, g), g, e[1])
                elif kind == "sums_before" and not first(t, g):
                    sums_over_keys(group(t, g) - 1)
                elif kind == "pv_before" and not first(t, g):
                    pv(t, group(t, g) - 1, (g - 1) % NG, 3)

            def pv(t, G, g, st):
                pe.wait_ge(exp_done, 16 * G + 4 * st + 4)
                if st == 0:
                    wait(pe, o_out, G)
                    if g == 0:
                        pe.wait_ge(c_free[1], use1(t, ("v_turn", 1)))
                for h in range(GH):
                    mm = nc.tensor.matmul(O_ps[HD * h:HD * (h + 1), :], v_sb[:, st, HD * g:HD * (g + 1)],
                                          probs[:, 4 * (st % 2) + h, :], start=(st == 0), stop=(st == ST - 1))
                mm.then_inc(pv_done, 1)

            def sums_over_keys(G):
                pe.wait_ge(acc_done, 12 * (G + 1))
                wait(pe, r_out, G)
                for h in range(GH):
                    mm = nc.tensor.matmul(R_ps[HD * h:HD * (h + 1), :], ones[:, :], acc[:, h, :],
                                          start=True, stop=True)
                mm.then_inc(sum_done, 1)

            walk(pe, do)
            pv(NB - 1, NB * NG - 1, NG - 1, 3)
            sums_over_keys(NB * NG - 1)

            pe.wait_ge(wo_lo_done, 16)

            def batch_rows(b, odd):
                d_hi, d_lo = halves(odd)
                pe.wait_ge(on_lo, NG * (b + 1))
                for lt in range(LT):
                    T = LT * b + lt
                    i = lt % 2
                    for c in range(2):
                        if isinstance(b, int) and b == 0 and lt < 2:
                            pe.wait_ge(exp_done, 16 * NG * NB)
                            pe.wait_ge(max_done, 16 * NG * NB)
                        else:
                            pe.wait_ge(y_added, 2 * (T - 2) + c + 1)
                        for k in range(KD):
                            for n, (o, w) in enumerate(((d_hi, w_lo), (d_lo, w_hi), (d_hi, w_hi))):
                                mm = nc.tensor.matmul(Y[2 * i + c][:, :], o[:, k, lt * P:(lt + 1) * P],
                                                      w[:, k, c * 512:(c + 1) * 512],
                                                      start=(k == 0 and n == 0), stop=(k == KD - 1 and n == 2))
                        mm.then_inc(y_full, 1)

            batch_rows(0, 0)
            batch_rows(1, 1)
            with pe.Fori(1, NB // 2) as p:
                batch_rows(2 * p, 0)
                batch_rows(2 * p + 1, 1)


_INS = ["x", "ctx_2048", "mask_Bx1xSxS2_ff0", "L0_xattn_Wq", "L0_xattn_bq", "L0_xattn_Wk", "L0_xattn_bk",
        "L0_xattn_Wv", "L0_xattn_bv", "L0_xattn_Wo", "L0_xattn_bo", "L0_xattn_gamma", "L0_xattn_beta"]


def kernel(**inputs):
    import numpy as _np
    import concourse.bacc as _bacc
    from concourse import mybir as _mybir
    from concourse.bass_utils import run_bass_kernel_spmd as _run

    nc = _bacc.Bacc("TRN2", target_bir_lowering=False, num_devices=1)
    arrays, args = {}, []
    for name in _INS:
        a = _np.ascontiguousarray(inputs[name])
        arrays[f"in_{name}_dram"] = a
        args.append(nc.dram_tensor(f"in_{name}_dram", a.shape, _mybir.dt.from_np(a.dtype), kind="ExternalInput").ap())
    shape = inputs["x"].shape
    args.append(nc.dram_tensor("out_0_dram", shape, _mybir.dt.float32, kind="ExternalOutput").ap())
    attention_kernel(nc, *args)
    r = _run(nc, [arrays], core_ids=[0])
    return r.results[0]["out_0_dram"]
```

```python
from contextlib import ExitStack

import concourse.bass as bass
from concourse import mybir

F32 = mybir.dt.float32
F32R = mybir.dt.float32r
ALU = mybir.AluOpType
ACT = mybir.ActivationFunctionType

P = 128
LOWEST = -3.4028234e38




HEAD = 7
TAIL = 8
FILL = 4
EXP_LAG = 1.5
SHIFT = (1.6, 2.2)
PROJECT = {1: range(24, 60), 2: range(60, 96), 4: range(120, 162), 5: range(162, 204), 6: range(204, 246),
           7: range(246, 288)}
MM_START = 0.2
STORE_LAG = 4.0
PV_LAG = 6.4
PV_BEFORE = 3.6
SUMS = (12.4, 14.0)
MASK = (9.5, 12.6)
TURNS = (7.6, 4.1)
TURNS_END = 28.0
X_LO = 1.1
O_PREP = (6.6, 3.3, 3.2)
Y_LAG = 3.0
RING = 5
TAKES = ("p1", "p2", "x_turn", "mask_turn", "v_turn", "shift_turn", "sums_before")
TAKER = {"x_hi": "x_turn", "x_lo": "x_turn", "mask_out": "mask_turn", "v_out": "v_turn", "shift_out": "shift_turn",
         "sums_out_before": "sums_before"}


def places(count):
    return [MM_START + (31.5 - MM_START) * n / (count - FILL) for n in range(count - FILL)] + [31.8] * FILL


def finished(g):
    if g in (0, 3):
        return [(4 * (g // 3), 31.8)]
    at = places(len(PROJECT[g]))
    return [(n // 24, at[n - PROJECT[g][0]]) for n in PROJECT[g] if n % 24 == 23]


def timeline(g, project, last):
    at = []

    def put(pos, *entry):
        at.append((pos, len(at), entry))

    more = not (last and g == 7)
    mixed = 32 - HEAD - TAIL
    inner = 16 - HEAD - TAIL
    p2_at = list(range(HEAD)) + [HEAD + (mixed * (n + 1)) // (inner + 1) - 1 for n in range(inner)] + \
        list(range(32 - TAIL, 32))
    p1_at = [pos for pos in range(32) if pos not in p2_at]
    for i, x in enumerate(p2_at):
        put(x, "p2", i)
        if x + EXP_LAG < 32:
            put(x + EXP_LAG, "exp", i, 0)
    for i, x in enumerate(p2_at):
        if x + EXP_LAG >= 32:
            put(x + EXP_LAG - 32, "exp", i, 1)
    if more:
        put(-0.5, "load_stack")
        for i, x in enumerate(p1_at):
            put(x, "p1", i)
        put(p1_at[-1] + 0.4, "shift_neg")
        put(p2_at[-TAIL] + SHIFT[0], "shift_turn")
        put(p2_at[-TAIL] + SHIFT[1], "shift_out")
    for st in range(3):
        put(min(p2_at[4 * st + 3] + PV_LAG, 31.6), "pv", st)
    put(PV_BEFORE, "pv_before")
    put(PV_BEFORE + 0.4, "out_before")
    put(SUMS[0], "sums_before")
    put(SUMS[1], "sums_out_before")
    if g == 1:
        put(20.0, "skip")
    if g == 0:
        for j in range(2):
            put(2.6 + 1.9 * j, "v_turn", j)
            put(3.8 + 1.0 * j, "v_out", j)
        for st in (2, 3):
            put(MASK[0] + 2.5 * (st - 2), "mask_turn", st)
            put(MASK[0] + 0.2 + 2.5 * (st - 2), "mask_out", st)
    if g == 6 and not last:
        put(31.0, "load_mask")
    if g == 7 and more:
        for st in (0, 1):
            put(MASK[1] + 4 * st, "mask_turn", st)
            put(MASK[1] + 0.2 + 4 * st, "mask_out", st)
    if project and g == 2:
        for d in range(2):
            put(20.0, "x_load", 1, d)
    if project and g in (0, 3):
        src = g // 3
        first = TURNS[src]
        gap = (TURNS_END - first) / 7
        if src == 0:
            for d in range(2):
                put(-0.4, "x_load", src, d)
        for d in range(8):
            x = first + gap * d
            put(x, "x_turn", src, d)
            if d + 2 < 8:
                put(x + 0.01, "x_load", src, d + 2)
            put(x + 0.2, "x_hi", src, d)
            put(x + X_LO, "x_lo", src, d)
            put(min(x + 4.6, 31.8), "mm", 4 * src, 3 * d, 3 * d + 3)
    if project and g in PROJECT:
        where, steps = places(len(PROJECT[g])), PROJECT[g]
        for n in range(0, len(steps), 2):
            put(where[n], "mm", steps[n] // 24, steps[n] % 24, steps[n] % 24 + 2)
    if project:
        for m, x in finished(g):
            if x < 30:
                put(x + 0.2, "keep", m, 0)
                put(x + 1.4, "split", m, 0)
            if x < 30 and x + 1.4 + STORE_LAG < 31:
                put(x + 1.4 + STORE_LAG, "store", m, 0)
    if project or g == 0:
        for m, x in finished((g - 1) % 8):
            if x >= 30:
                put(0.2, "keep", m, 1 if g == 0 else 0)
                put(1.2, "split", m, 1 if g == 0 else 0)
            if x >= 30 or x + 1.4 + STORE_LAG >= 31:
                put(1.2 + STORE_LAG if x >= 30 else max(x + 1.4 + STORE_LAG - 32, 0.1), "store", m, 1 if g == 0 else 0)
    if last and g in (1, 2, 3, 4):
        for n in range(4):
            k = 4 * (g - 1) + n
            if k == 0:
                put(0.3, "wo_load", 0)
                put(0.3, "wo_load", 1)
            put(4.5 + 7 * n, "wo_hi_lo", k)
            if k + 2 < 16:
                put(6.5 + 7 * n, "wo_load", k + 2)
    if last and g == 1:
        put(3.5, "recip_load")
    if last and g in (2, 3, 4, 5):
        put(9.5, "recip", g - 2)
    if last and g == 6:
        put(3.5, "recip_store")
    if last and g == 7:
        for n in range(8):
            put(-0.3 if n < 4 else O_PREP[0] + O_PREP[1] * (n - 4) + O_PREP[2] + 0.1, "o_load", n)
            put(O_PREP[0] + O_PREP[1] * n, "o_norm", n)
            put(O_PREP[0] + O_PREP[1] * n + 0.4, "o_hi", n)
            put(O_PREP[0] + O_PREP[1] * n + O_PREP[2], "o_lo", n)
            if O_PREP[0] + O_PREP[1] * n + O_PREP[2] + Y_LAG < 32:
                put(O_PREP[0] + O_PREP[1] * n + O_PREP[2] + Y_LAG, "y", n)
    return [e for _, _, e in sorted(at, key=lambda x: (x[0], x[1]))]


class Ring:

    def __init__(self):
        self.at = 0
        self.had = [None] * RING
        self.before = {}

    def step(self, entries, no_sums=False):
        got, bank = [], {}
        for e in entries:
            if e[0] == "skip" or e[0] == "sums_before" and no_sums:
                self.at = (self.at + 1) % RING
            if e[0] in TAKES and not (e[0] == "sums_before" and no_sums):
                got.append(e + (self.at, self.had[self.at]))
                bank[e], self.had[self.at] = self.at, (e, 0)
                self.at = (self.at + 1) % RING
            elif e[0] == "exp":
                got.append(e + ((self.before if e[2] else bank).get(("p2", e[1])),))
            elif e[0] in TAKER:
                got.append(e + (bank.get((TAKER[e[0]],) + e[1:]),))
            else:
                got.append(e)
        self.had = [h and (h[0], h[1] + 1) for h in self.had]
        self.before = bank
        return got


def prologue():
    at = [("x_load", 0, 0), ("w_load", 0), ("x_load", 0, 1), ("w_load", 1), ("w_load", 2)]
    for src in range(2):
        for d in range(8):
            at.append(("x_turn", src, d))
            if d + 2 < 8:
                at.append(("x_load", src, d + 2))
            elif src == 0:
                at.append(("x_load", 1, d - 6))
            at.append(("x_hi", src, d))
            if src == 0:
                at += [("w_split", d), ("w_load", d + 3)]
                if d == 5:
                    at.append(("bias_load",))
            at.append(("x_lo", src, d))
            if d > 0:
                at.append(("mm", 4 * src, 3 * d - 3, 3 * d))
        at.append(("mm", 4 * src, 21, 24))
        if src == 0:
            at += [("w_load", n) for n in range(11, 16)] + [("load_mask",), ("biases",)]
        at += [("keep", 4 * src, 0), ("split", 4 * src, 0), ("store", 4 * src, 0)]
        if src == 1:
            at.append(("load_stack",))
        for m in (range(1, 4) if src == 0 else range(5, 12)):
            if src == 0:
                for k in range(8 + 6 * (m - 1), min(8 + 6 * m, 24)):
                    at.append(("w_split", k))
                    if k + 8 < 24:
                        at.append(("w_load", k + 8))
            if m == 11:
                at += [("mm", m, 0, 8), ("shift_turn",), ("shift_out",), ("mm", m, 8, 24)]
            else:
                at.append(("mm", m, 0, 24))
            at += [("keep", m, 0), ("split", m, 0), ("store", m, 0)]
            if m in (5, 6):
                at += [("mask_turn", m - 5), ("mask_out", m - 5)]
            if m >= 7:
                at += [("p1", i) for i in range(4 * (m - 7), min(4 * (m - 6), 16))]
            if m == 10:
                at.append(("shift_neg",))
    return at


def attention_kernel(nc, x, ctx, mask, wq, bq, wk, bk, wv, bv, wo, bo, gamma, beta, out):
    B, L, D = x.shape
    S = ctx.shape[1]
    KV = wk.shape[1]
    HD = 32
    NG = KV // HD
    GH = D // KV
    KD = D // P
    LT, ST = L // P, S // P
    SCALE = float(HD) ** -0.5
    EPS = 1e-6
    NB = B
    assert (L, S, GH * HD, NG, KD) == (512, 512, P, 8, 8)

    ring = Ring()
    FIRST = ring.step(prologue())
    begin = ring.at
    START = ring.step(timeline(0, True, False), no_sums=True)
    STEPS = [START] + [ring.step(timeline(g, True, False)) for g in range(1, NG)]
    assert ring.at == begin
    STEPS[0] = ring.step(timeline(0, True, False))
    for g in range(1, NG):
        assert STEPS[g] == ring.step(timeline(g, True, False))
    LAST = [ring.step(timeline(g, False, True)) for g in range(NG)]
    AFTER = ring.step([("exp", i, 1) for i in range(16 - int(EXP_LAG), 16)] + [("sums_before",), ("sums_out_before",)])

    with ExitStack() as stack:
        def sb(name, shape, dt, where=stack):
            return where.enter_context(nc.sbuf_tensor(name, shape, dt))

        def sem(name):
            return stack.enter_context(nc.semaphore(name))

        def dram(name, shape, dt):
            return nc.dram_tensor(name, shape, dt, kind="Internal").ap()

        q_hi_d = dram("q_hi_d", [NB * NG, P, L], F32)
        q_lo_d = dram("q_lo_d", [NB * NG, P, L], F32)
        k_hi_d = dram("k_hi_d", [NB * 2, P, S], F32)
        k_lo_d = dram("k_lo_d", [NB * 2, P, S], F32)
        o_d = dram("o_d", [NB * NG, P, L], F32)
        r_d = dram("r_d", [NB * NG, GH, L], F32)
        ri_d = dram("ri_d", [NB * NG, GH, L], F32)

        w_hi = sb("w_hi", [P, KD, D + 2 * KV], F32R)
        w_lo = sb("w_lo", [P, KD, D + 2 * KV], F32R)
        xT_hi = sb("xT_hi", [P, KD, L], F32R)
        xT_lo = sb("xT_lo", [P, KD, L], F32R)
        x_raw = sb("x_raw", [P, 2, L], F32)
        ident = sb("ident", [P, P], F32)
        ones = sb("ones", [P, HD], F32)
        bq_c = sb("bq_c", [P, NG], F32)
        bq_s = sb("bq_s", [P, NG], F32)
        bkv_c = sb("bkv_c", [P, 4], F32)
        eps_c = sb("eps_c", [P, 1], F32)
        row_max = sb("row_max", [P, 4 * GH], F32)
        shift = sb("shift", [P, 2 * 4 * GH], F32R)
        shift_rows = sb("shift_rows", [2 * 4 * GH, P], F32R)
        vT_sb = sb("vT_sb", [P, 2, S], F32)
        sums = vT_sb[:, :, :].rearrange("p a s -> p (a s)")
        assert NG * NB * GH * L // P == 2 * S
        EARLY = NG * (NB - 1) * GH * L // P
        with ExitStack() as first_part:
            def sb1(name, shape, dt):
                return sb(name, shape, dt, first_part)

            mask_l = sb1("mask_l", [P, LT, S], F32)
            q_stack = [sb1("q_stack0", [98, GH, L], F32R)]
            mask_s = sb1("mask_s", [P, ST, L], F32)
            q_stack.append(sb1("q_stack1", [98, GH, L], F32R))
            probs = sb1("probs", [P, 8, L], F32)
            k_stack = [sb1(f"k_stack{i}", [98, S], F32R) for i in range(2)]
            v_sb = sb1("v_sb", [P, ST, KV], F32)
            part = sb1("part", [P, L], F32)
            part_hi = sb1("part_hi", [P, L], F32R)
            acc = sb1("acc", [P, GH, L], F32)
            out_sb = sb1("out_sb", [P, L], F32)
        o_raw = sb("o_raw", [P, 4, L], F32)
        r_inv = sb("r_inv", [P, 4, L], F32)
        x_res = sb("x_res", [P, 2, D], F32)
        y_sb = sb("y_sb", [P, 2, D], F32)
        z_sb = sb("z_sb", [P, 2, D], F32)
        bo_b = sb("bo_b", [P, D], F32)
        gamma_b = sb("gamma_b", [P, D], F32)
        beta_b = sb("beta_b", [P, D], F32)
        stats = sb("stats", [P, 2, 6], F32)
        mean_var = sb("mean_var", [P, 2], F32)
        std = sb("std", [P, 1], F32)
        rstd = sb("rstd", [P, 1], F32)

        bank = [stack.enter_context(nc.psum_tensor(f"bank{i}", [P, 512], F32)) for i in range(8)]
        S, O_ps, C = bank[0:RING], bank[RING], bank[6:8]
        Y = C + [b for n, b in enumerate(S) if n != AFTER[-2][1]][0:2]

        consts_ready = sem("consts_ready")
        biases_in = sem("biases_in")
        bias_scaled = sem("bias_scaled")
        w_in = [sem(f"w_in{i}") for i in range(8)]
        w_hi_done, w_lo_done = sem("w_hi_done"), sem("w_lo_done")
        x_in = [sem("x_in0"), sem("x_in1")]
        c_full = [sem("c_full0"), sem("c_full1")]
        c_free = [sem("c_free0"), sem("c_free1")]
        x_turned, v_turned, mask_turned, shift_turned = (sem(n) for n in ("x_turned", "v_turned", "mask_turned",
                                                                         "shift_turned"))
        x_lo_done, v_out, mask_out, shift_out = (sem(n) for n in ("x_lo_done", "v_out", "mask_out", "shift_out"))
        x_hi_done = sem("x_hi_done")
        part_hi_done, part_lo_done = sem("part_hi_done"), sem("part_lo_done")
        qk_stored = sem("qk_stored")
        mask_in = sem("mask_in")
        stack_in = sem("stack_in")
        p1_done, max_done = sem("p1_done"), sem("max_done")
        neg_hi, neg_lo = sem("neg_hi"), sem("neg_lo")
        shift_in = sem("shift_in")
        p2_done, masked, exp_done = sem("p2_done"), sem("masked"), sem("exp_done")
        pv_done = sem("pv_done")
        acc_done, sum_done = sem("acc_done"), sem("sum_done")
        o_out, r_out, out_stored = sem("o_out"), sem("r_out"), sem("out_stored")
        wo_in = [sem("wo_in0"), sem("wo_in1")]
        wo_hi_done, wo_lo_done = sem("wo_hi_done"), sem("wo_lo_done")
        r_in, r_done, ri_stored = sem("r_in"), sem("r_done"), sem("ri_stored")
        rows_in = sem("rows_in")
        o_in = [sem(f"o_in{i}") for i in range(4)]
        normed, on_hi, on_lo = sem("normed"), sem("on_hi"), sem("on_lo")
        res_in = [sem("res_in0"), sem("res_in1")]
        res_bo = sem("res_bo")
        y_full, y_added = sem("y_full"), sem("y_added")
        y_stat, y_mv, y_std, y_rstd, y_cen = (sem(n) for n in ("y_stat", "y_mv", "y_std", "y_rstd", "y_cen"))
        z_done = sem("z_done")
        z_stored = [sem("z_stored0"), sem("z_stored1")]

        SPLITS = [0, 1, 4, 5, 6, 7, 8, 9, 10, 11]

        def x_no(t, src, d):
            return 2 * KD * (t + 1) + KD * src + d + 1

        def split_no(t, m):
            return 10 * (t + 1) + SPLITS.index(m) + 1

        def wait(eng, s, value):
            if not (isinstance(value, int) and value <= 0):
                eng.wait_ge(s, value)

        def counted_ahead(eng, *values):
            for v in values:
                if not isinstance(v, int):
                    eng.lower_val(v)

        def walk(eng, do):
            for e in FIRST:
                do(-1, NG - 1, e)
            for g in range(NG):
                for e in START if g == 0 else STEPS[g]:
                    do(0, g, e)
            with eng.Fori(1, NB - 1) as t:
                for g in range(NG):
                    for e in STEPS[g]:
                        do(t, g, e)
            for g in range(NG):
                for e in LAST[g]:
                    do(NB - 1, g, e)

        def group(t, g):
            return NG * t + g

        def first(t, g):
            return isinstance(t, int) and t == 0 and g == 0

        def made_before(t, e):
            return isinstance(t, int) and t == 0 and e[2] == 1

        def tile_no(t, m):
            return 6 * (t + 1) + m // 2 + 1

        W_ORDER = list(range(16, 24)) + list(range(16))

        def w_place(n):
            return (n // 2, (n % 2) * 512) if n < 16 else (n - 16, D)

        def rows_of(a, part):
            cut = NG * (NB - 1)
            r = (a[0:cut] if part == 0 else a[cut:NG * NB]).rearrange("g h l -> (g h l)")
            return r.rearrange("(p f) -> p f", p=P)

        def halves(odd):
            if odd:
                return w_hi[:, :, D:D + 512], w_lo[:, :, D:D + 512]
            return xT_hi[:, :, :], xT_lo[:, :, :]

        block = stack.enter_context(nc.Block())

        @block.sync
        def _(sp):
            def w_piece(n):
                if n < 16:
                    return [(slice(0, 512), wq[(n // 2) * P:(n // 2 + 1) * P, (n % 2) * 512:(n % 2 + 1) * 512])]
                k = n - 16
                return [(slice(0, KV), wk[k * P:(k + 1) * P, :]), (slice(KV, 2 * KV), wv[k * P:(k + 1) * P, :])]

            def do(t, g, e):
                kind = e[0]
                if kind == "w_load":
                    k = e[1]
                    wait(sp, w_lo_done, k - 7)
                    for cols, src in w_piece(W_ORDER[k]):
                        sp.dma_start(probs[:, k % 8, cols], src).then_inc(w_in[k % 8], 16)
                elif kind == "bias_load":
                    with nc.allow_non_contiguous_dma(reason="bias columns, once"):
                        sp.dma_start(bq_c[:, :], bq.rearrange("(g p) -> p g", p=P)).then_inc(biases_in, 16)
                        sp.dma_start(bkv_c[:, 0:2], bk.rearrange("(g p) -> p g", p=P)).then_inc(biases_in, 16)
                        sp.dma_start(bkv_c[:, 2:4], bv.rearrange("(g p) -> p g", p=P)).then_inc(biases_in, 16)
                elif kind == "x_load":
                    src, d = e[1], e[2]
                    wait(sp, x_turned, x_no(t, src, d) - 2)
                    dram_in = (ctx, x)[src][t + 1].rearrange("(a p) d -> p a d", p=P)[:, :, d * P:(d + 1) * P]
                    sp.dma_start(x_raw[:, d % 2, :].rearrange("p (a d) -> p a d", a=LT), dram_in)\
                      .then_inc(x_in[d % 2], 16)
                elif kind == "load_mask":
                    wait(sp, max_done, 128 * (t + 1))
                    sp.dma_start(mask_l[:, :, :], mask[t + 1, 0].rearrange("(a p) s -> p a s", p=P))\
                      .then_inc(mask_in, 16)
                elif kind == "store" and e[1] not in (2, 3) and not made_before(t, e):
                    m, nt = e[1], t - e[2]
                    sp.wait_ge(part_lo_done, split_no(nt, m))
                    hi_dst, lo_dst = (k_hi_d, k_lo_d) if m < 2 else (q_hi_d, q_lo_d)
                    row = 2 * (nt + 1) + m if m < 2 else NG * (nt + 1) + m - 4
                    sp.dma_start(hi_dst[row], part_hi[:, :].bitcast(F32)).then_inc(qk_stored, 16)
                    sp.dma_start(lo_dst[row], part[:, :]).then_inc(qk_stored, 16)
                elif kind == "load_stack":
                    G = group(t, g) + 1
                    b = (g + 1) % 2
                    nt, ng = (t, g + 1) if g + 1 < NG else (t + 1, 0)
                    counts = 16 * (G - 1), 32 * split_no(nt - 1, 4 + ng)
                    counted_ahead(sp, *counts)
                    wait(sp, p2_done, counts[0])
                    wait(sp, qk_stored, counts[1])
                    q_hi, q_lo = (a[G].rearrange("(h d) l -> d h l", h=GH) for a in (q_hi_d, q_lo_d))
                    kr = 2 * nt + ng // 4
                    k0 = HD * (ng % 4)
                    k_hi, k_lo = (a[kr][k0:k0 + HD, :] for a in (k_hi_d, k_lo_d))
                    for i, (q, k) in enumerate(((q_hi, k_hi), (q_lo, k_hi), (q_hi, k_lo))):
                        sp.dma_start(k_stack[b][HD * i:HD * (i + 1), :].bitcast(F32), k).then_inc(stack_in, 16)
                        sp.dma_start(q_stack[b][HD * i:HD * (i + 1), :, :].bitcast(F32), q).then_inc(stack_in, 16)
                elif kind == "shift_out":
                    G = group(t, g) + 1
                    b = (g + 1) % 2
                    wait(sp, shift_out, G + 1)
                    for r in range(2):
                        sp.dma_start(q_stack[b][96 + r:97 + r, :, :].bitcast(F32),
                                     shift_rows[16 * r:16 * (r + 1), :].bitcast(F32)).then_inc(shift_in, 16)
                elif kind == "out_before" and not first(t, g):
                    store_o(group(t, g) - 1)
                elif kind == "sums_out_before" and not first(t, g):
                    store_r(group(t, g) - 1)
                elif kind == "wo_load":
                    n = e[1]
                    if n >= 2:
                        sp.wait_ge(wo_lo_done, n - 1)
                    sp.dma_start(x_raw[:, n % 2, :], wo[(n // 2) * P:(n // 2 + 1) * P,
                                                        (n % 2) * 512:(n % 2 + 1) * 512]).then_inc(wo_in[n % 2], 16)
                elif kind == "recip_load":
                    sp.wait_ge(out_stored, 32 * NG * (NB - 1))
                    sp.wait_ge(v_turned, 2 * NB)
                    sp.dma_start(sums[:, 0:EARLY], rows_of(r_d, 0)).then_inc(r_in, 16)
                elif kind == "recip_store":
                    sp.wait_ge(r_done, 4)
                    sp.dma_start(rows_of(ri_d, 0), sums[:, 0:EARLY]).then_inc(ri_stored, 16)
                elif kind == "o_load":
                    if e[1] == 0:
                        sp.wait_ge(ri_stored, 16)
                        sp.wait_ge(max_done, 16 * NG * NB)
                        sp.wait_ge(p2_done, 16 * (NG * NB - 1))
                    load_o(0, e[1])

            def store_o(G):
                sp.wait_ge(o_out, G + 1)
                sp.dma_start(o_d[G], out_sb[:, :]).then_inc(out_stored, 16)

            def store_r(G):
                sp.wait_ge(r_out, G + 1)
                sp.dma_start(r_d[G], out_sb[0:P:HD, :]).then_inc(out_stored, 16)

            def load_o(b, g):
                n = NG * b + g
                wait(sp, on_lo, n - 3)
                sp.dma_start(o_raw[:, g % 4, :], o_d[n]).then_inc(o_in[g % 4], 16)
                for h in range(GH):
                    sp.dma_start(r_inv[HD * h:HD * (h + 1), g % 4, :],
                                 ri_d[n][h:h + 1, :].broadcast_to([HD, L])).then_inc(o_in[g % 4], 16)

            def load_res(b, lt):
                T = LT * b + lt
                wait(sp, y_added, 2 * (T - 1))
                sp.dma_start(x_res[:, lt % 2, :], x[b, lt * P:(lt + 1) * P, :]).then_inc(res_in[lt % 2], 16)

            walk(sp, do)
            sp.wait_ge(masked, 16 * NG * NB)
            load_res(0, 0)
            load_res(0, 1)
            load_o(1, 0)
            load_o(1, 1)
            store_o(NB * NG - 1)
            store_r(NB * NG - 1)
            sp.dma_start(bo_b[:, :], bo.rearrange("(a d) -> a d", a=1).broadcast_to([P, D])).then_inc(rows_in, 16)
            sp.dma_start(gamma_b[:, :], gamma.rearrange("(a d) -> a d", a=1).broadcast_to([P, D])).then_inc(rows_in, 16)
            sp.dma_start(beta_b[:, :], beta.rearrange("(a d) -> a d", a=1).broadcast_to([P, D])).then_inc(rows_in, 16)

            def store(b, lt):
                T = LT * b + lt
                sp.wait_ge(z_done, T + 1)
                sp.dma_start(out[b, lt * P:(lt + 1) * P, :], z_sb[:, lt % 2, :]).then_inc(z_stored[lt % 2], 16)

            sp.wait_ge(out_stored, 32 * NG * NB)
            sp.dma_start(sums[:, EARLY:], rows_of(r_d, 1)).then_inc(r_in, 16)

            def batch_rows(b, more, further):
                for lt in range(LT):
                    if lt < 3 and more:
                        load_o(b + 1, 2 * lt + 2)
                        load_o(b + 1, 2 * lt + 3)
                    if lt == 3 and further:
                        load_o(b + 2, 0)
                        load_o(b + 2, 1)
                    store(b, lt)
                    if lt >= 2 and more:
                        load_res(b + 1, lt - 2)
                    elif lt < 2:
                        load_res(b, lt + 2)

            batch_rows(0, True, True)
            sp.wait_ge(r_done, 5)
            sp.dma_start(rows_of(ri_d, 1), sums[:, EARLY:]).then_inc(ri_stored, 16)
            sp.wait_ge(ri_stored, 32)
            with sp.Fori(1, NB - 2) as b:
                batch_rows(b, True, True)
            batch_rows(NB - 2, True, False)
            batch_rows(NB - 1, False, False)
            sp.wait_ge(z_stored[0], 16 * 2 * NB)
            sp.wait_ge(z_stored[1], 16 * 2 * NB)

        @block.gpsimd
        def _(pool):
            nc.gpsimd.memset(ident[:, :], 0.0).then_inc(consts_ready, 1)
            nc.gpsimd.memset(ones[:, :], 1.0).then_inc(consts_ready, 1)
            nc.gpsimd.memset(eps_c[:, :], EPS).then_inc(consts_ready, 1)
            for i in range(2):
                pool.wait_ge(consts_ready, 3 + i)
                nc.gpsimd.memset(k_stack[i][96:98, :].bitcast(F32), 1.0).then_inc(consts_ready, 1)
            pool.wait_ge(consts_ready, 5)
            nc.gpsimd.affine_select(out=ident[:, :], in_=ident[:, :], compare_op=ALU.not_equal, fill=1.0, base=0,
                                    pattern=[[-1, P]], channel_multiplier=1).then_inc(consts_ready, 1)

            def do(t, g, e):
                kind = e[0]
                if kind == "split" and e[1] not in (2, 3) and not made_before(t, e):
                    pool.wait_ge(part_hi_done, split_no(t - e[2], e[1]))
                    nc.gpsimd.tensor_tensor(part[:, :], part[:, :], part_hi[:, :].bitcast(F32), ALU.subtract)\
                      .then_inc(part_lo_done, 1)
                elif kind == "exp" and e[1] >= 4 and not (first(t, g) and e[2]):
                    add_up(group(t, g) - e[2], e[1])
                elif kind == "wo_hi_lo":
                    n = e[1]
                    pool.wait_ge(wo_hi_done, n + 1)
                    k, c = n // 2, (n % 2) * 512
                    nc.gpsimd.tensor_tensor(w_lo[:, k, c:c + 512], x_raw[:, n % 2, :],
                                            w_hi[:, k, c:c + 512].bitcast(F32), ALU.subtract).then_inc(wo_lo_done, 1)

            def add_up(G, i):
                st, h = i // 4, i % 4
                if st == 1 and h == 0:
                    wait(pool, sum_done, G)
                if st >= 2:
                    pool.wait_ge(acc_done, 12 * G + 4 * (st - 2) + h + 1)
                pool.wait_ge(exp_done, 16 * G + i + 1)
                nc.gpsimd.tensor_tensor(acc[:, h, :], probs[:, h, :] if st == 1 else acc[:, h, :],
                                        probs[:, 4 * (st % 2) + h, :], ALU.add).then_inc(acc_done, 1)

            walk(pool, do)
            for i in range(16 - int(EXP_LAG), 16):
                add_up(NB * NG - 1, i)

            def lo(b, g, odd):
                n = NG * b + g
                _, d_lo = halves(odd)
                d_hi, _ = halves(odd)
                pool.wait_ge(on_hi, n + 1)
                nc.gpsimd.tensor_tensor(d_lo[:, g, :], o_raw[:, g % 4, :], d_hi[:, g, :].bitcast(F32),
                                        ALU.subtract).then_inc(on_lo, 1)

            def residual(b, lt):
                T = LT * b + lt
                pool.wait_ge(res_in[lt % 2], 16 * (2 * b + lt // 2 + 1))
                nc.gpsimd.tensor_tensor(x_res[:, lt % 2, :], x_res[:, lt % 2, :], bo_b[:, :], ALU.add)\
                  .then_inc(res_bo, 1)

            pool.wait_ge(rows_in, 48)

            def batch_rows(b, odd, more):
                for lt in range(LT):
                    residual(b, lt)
                    if more:
                        lo(b + 1, 2 * lt, 1 - odd)
                        lo(b + 1, 2 * lt + 1, 1 - odd)

            with pool.Fori(0, NB // 2 - 1) as p:
                batch_rows(2 * p, 0, True)
                batch_rows(2 * p + 1, 1, True)
            batch_rows(NB - 2, 0, True)
            batch_rows(NB - 1, 1, False)

        @block.scalar
        def _(act):
            def do(t, g, e):
                kind = e[0]
                if kind == "w_split":
                    k = e[1]
                    n = W_ORDER[k]
                    act.wait_ge(w_in[k % 8], 32 + 16 * (k // 8))
                    d, c = w_place(n)
                    nc.scalar.activation(w_hi[:, d, c:c + 512], probs[:, k % 8, :], ACT.Copy).then_inc(w_hi_done, 1)
                elif kind == "biases":
                    act.wait_ge(biases_in, 48)
                    nc.scalar.mul(bq_s[:, :], bq_c[:, :], SCALE).then_inc(bias_scaled, 1)
                    act.wait_ge(bias_scaled, 1)
                elif kind == "x_hi":
                    src, d = e[1], e[2]
                    act.wait_ge(x_turned, x_no(t, src, d))
                    nc.scalar.activation(xT_hi[:, d, :], S[e[3]][:, :], ACT.Copy).then_inc(x_hi_done, 1)
                elif kind == "keep" and not made_before(t, e):
                    m, nt = e[1], t - e[2]
                    c = m % 2
                    act.wait_ge(c_full[c], tile_no(nt, m))
                    if m in (2, 3):
                        nc.scalar.activation(vT_sb[:, m - 2, :], C[c][:, :], ACT.Identity, bias=bkv_c[:, m:m + 1])\
                          .then_inc(c_free[c], 1)
                    else:
                        wait(act, qk_stored, 32 * (split_no(nt, m) - 1))
                        scale, bias = (1.0, bkv_c[:, m:m + 1]) if m < 2 else (SCALE, bq_s[:, m - 4:m - 3])
                        nc.scalar.activation(part[:, :], C[c][:, :], ACT.Identity, scale=scale, bias=bias)\
                          .then_inc(c_free[c], 1)
                elif kind == "split" and e[1] not in (2, 3) and not made_before(t, e):
                    act.wait_ge(c_free[e[1] % 2], tile_no(t - e[2], e[1]))
                    nc.scalar.activation(part_hi[:, :], part[:, :], ACT.Copy).then_inc(part_hi_done, 1)
                elif kind == "v_out":
                    j = e[1]
                    act.wait_ge(v_turned, 2 * t + j + 1)
                    wait(act, pv_done, 4 * NG * t)
                    nc.scalar.activation(v_sb[:, :, j * P:(j + 1) * P],
                                         S[e[2]][:, :].rearrange("p (s d) -> p s d", s=ST), ACT.Copy)\
                      .then_inc(v_out, 1)
                elif kind == "mask_out":
                    st = e[1]
                    nt = t + 1 if g == 7 else t
                    act.wait_ge(mask_turned, 4 * nt + st + 1)
                    wait(act, masked, 128 * nt - 16 + 4 * st + 4 if not (isinstance(nt, int) and nt == 0) else 0)
                    nc.scalar.activation(mask_s[:, st, :], S[e[2]][:, :], ACT.Copy).then_inc(mask_out, 1)
                elif kind == "shift_out":
                    G = group(t, g) + 1
                    act.wait_ge(shift_turned, G + 1)
                    wait(act, shift_in, 32 * G)
                    nc.scalar.activation(shift_rows[:, :], S[e[1]][0:32, 0:P], ACT.Copy).then_inc(shift_out, 1)
                elif kind == "o_hi":
                    hi(0, e[1], 0)
                elif kind == "exp" and not (first(t, g) and e[2]):
                    exp(group(t, g) - e[2], e[1], e[3])
                elif kind == "out_before" and not first(t, g):
                    out_o(group(t, g) - 1)
                elif kind == "sums_out_before" and not first(t, g):
                    out_r(group(t, g) - 1, e[1])
                elif kind == "wo_hi_lo":
                    n = e[1]
                    act.wait_ge(wo_in[n % 2], 16 * (n // 2 + 1))
                    k, c = n // 2, (n % 2) * 512
                    act.wait_ge(c_full[1], tile_no(NB - 2, 11))
                    nc.scalar.activation(w_hi[:, k, c:c + 512], x_raw[:, n % 2, :], ACT.Copy).then_inc(wo_hi_done, 1)

            def hi(b, g, odd):
                n = NG * b + g
                d_hi, _ = halves(odd)
                act.wait_ge(normed, n + 1)
                wait(act, y_full, 8 * (b - 1) if not (isinstance(b, int) and b == 0) else 0)
                nc.scalar.activation(d_hi[:, g, :], o_raw[:, g % 4, :], ACT.Copy).then_inc(on_hi, 1)

            def exp(G, i, bank_no):
                act.wait_ge(masked, 16 * G + i + 1)
                st, h = i // 4, i % 4
                wait(act, pv_done, 4 * G + st - 1)
                wait(act, acc_done, 12 * G + (h - 7, h - 3, h + 1, h + 1)[st])
                nc.scalar.activation(probs[:, i % 8, :], S[bank_no][:, :], ACT.Exp).then_inc(exp_done, 1)

            def out_o(G):
                act.wait_ge(pv_done, 4 * (G + 1))
                wait(act, out_stored, 32 * G)
                nc.scalar.activation(out_sb[:, :], O_ps[:, :], ACT.Copy).then_inc(o_out, 1)

            def out_r(G, bank_no):
                act.wait_ge(sum_done, G + 1)
                act.wait_ge(out_stored, 32 * G + 16)
                nc.scalar.activation(out_sb[:, :], S[bank_no][:, :], ACT.Copy).then_inc(r_out, 1)

            walk(act, do)
            for e in AFTER[:-2]:
                exp(NB * NG - 1, e[1], e[3])
            out_o(NB * NG - 1)
            out_r(NB * NG - 1, AFTER[-1][1])

            def root(b, lt):
                T = LT * b + lt
                act.wait_ge(y_mv, T + 1)
                nc.scalar.activation(std[:, :], mean_var[:, 1:2], ACT.Sqrt, bias=eps_c[:, :]).then_inc(y_std, 1)


            def batch_rows(b, odd, more):
                for lt in range(LT):
                    if more:
                        hi(b + 1, 2 * lt, 1 - odd)
                        hi(b + 1, 2 * lt + 1, 1 - odd)
                    root(b, lt)

            batch_rows(0, 0, True)
            batch_rows(1, 1, True)
            with act.Fori(1, NB // 2 - 1) as p:
                batch_rows(2 * p, 0, True)
                batch_rows(2 * p + 1, 1, True)
            batch_rows(NB - 2, 0, True)
            batch_rows(NB - 1, 1, False)

        @block.vector
        def _(dve):
            def do(t, g, e):
                kind = e[0]
                if kind == "w_split":
                    k = e[1]
                    dve.wait_ge(w_hi_done, k + 1)
                    d, c = w_place(W_ORDER[k])
                    nc.vector.tensor_tensor(w_lo[:, d, c:c + 512], probs[:, k % 8, :],
                                            w_hi[:, d, c:c + 512].bitcast(F32), ALU.subtract).then_inc(w_lo_done, 1)
                elif kind == "x_lo":
                    src, d = e[1], e[2]
                    dve.wait_ge(x_hi_done, x_no(t, src, d))
                    nc.vector.tensor_tensor(xT_lo[:, d, :], S[e[3]][:, :], xT_hi[:, d, :].bitcast(F32),
                                            ALU.subtract).then_inc(x_lo_done, 1)
                elif kind == "p1":
                    i = e[1]
                    n = 16 * (group(t, g) + 1) + i
                    h, lt = i // 4, i % 4
                    if i == 0:
                        dve.wait_ge(mask_in, 16 * (t + 2) if g == 7 else 16 * (t + 1))
                    counted_ahead(dve, n + 1)
                    dve.wait_ge(w_hi_done, 24)
                    dve.wait_ge(p1_done, n + 1)
                    nc.vector.tensor_tensor_reduce(out=S[e[2]][:, :], in0=S[e[2]][:, :], in1=mask_l[:, lt, :],
                                                   scale=1.0, scalar=LOWEST, op0=ALU.add, op1=ALU.max,
                                                   accum_out=row_max[:, i:i + 1]).then_inc(max_done, 1)
                elif kind == "shift_neg":
                    G = group(t, g) + 1
                    dve.wait_ge(max_done, 16 * (G + 1))
                    wait(dve, shift_turned, G)
                    nc.vector.tensor_scalar(shift[:, 0:16], row_max[:, :], -1.0, None, ALU.mult).then_inc(neg_hi, 1)
                    dve.wait_ge(neg_hi, G + 1)
                    nc.vector.scalar_tensor_tensor(out=shift[:, 16:32], in0=row_max[:, :], scalar=-1.0,
                                                   in1=shift[:, 0:16].bitcast(F32), op0=ALU.mult, op1=ALU.subtract)\
                      .then_inc(neg_lo, 1)
                elif kind == "p2":
                    i = e[1]
                    st = i // 4
                    n = 16 * group(t, g) + i
                    if g == 0 and i % 4 == 0:
                        dve.wait_ge(mask_out, 4 * t + st + 1)
                    dve.wait_ge(p2_done, n + 1)
                    nc.vector.tensor_tensor(S[e[2]][:, :], S[e[2]][:, :], mask_s[:, st, :], ALU.add)\
                      .then_inc(masked, 1)
                elif kind == "recip":
                    dve.wait_ge(r_in, 16)
                    a, b = EARLY * e[1] // 4, EARLY * (e[1] + 1) // 4
                    nc.vector.reciprocal(sums[:, a:b], sums[:, a:b]).then_inc(r_done, 1)
                elif kind == "o_norm":
                    norm(0, e[1])
                elif kind == "o_lo":
                    k = e[1]
                    dve.wait_ge(on_hi, k + 1)
                    nc.vector.tensor_tensor(xT_lo[:, k, :], o_raw[:, k % 4, :], xT_hi[:, k, :].bitcast(F32),
                                            ALU.subtract).then_inc(on_lo, 1)

            def norm(b, g):
                n = NG * b + g
                dve.wait_ge(o_in[g % 4], 80 * (2 * b + g // 4 + 1))
                nc.vector.tensor_tensor(o_raw[:, g % 4, :], o_raw[:, g % 4, :], r_inv[:, g % 4, :], ALU.mult)\
                  .then_inc(normed, 1)

            walk(dve, do)

            def rows(b, lt):
                T = LT * b + lt
                i = lt % 2
                dve.wait_ge(res_bo, T + 1)
                for c in range(2):
                    dve.wait_ge(y_full, 2 * T + c + 1)
                    nc.vector.tensor_tensor(y_sb[:, i, c * 512:(c + 1) * 512], Y[2 * i + c][:, :],
                                            x_res[:, i, c * 512:(c + 1) * 512], ALU.add).then_inc(y_added, 1)
                for c in range(2):
                    dve.wait_ge(y_added, 2 * T + c + 1)
                    nc.vector.bn_stats(stats[:, c, :], y_sb[:, i, c * 512:(c + 1) * 512]).then_inc(y_stat, 1)
                dve.wait_ge(wo_hi_done, 16)
                dve.wait_ge(y_stat, 2 * T + 2)
                nc.vector.bn_aggr(mean_var[:, :], stats[:, :, :]).then_inc(y_mv, 1)
                dve.wait_ge(y_mv, T + 1)
                wait(dve, z_stored[i], 16 * (2 * b + lt // 2))
                nc.vector.scalar_tensor_tensor(out=z_sb[:, i, :], in0=y_sb[:, i, :], scalar=mean_var[:, 0:1],
                                               in1=gamma_b[:, :], op0=ALU.subtract, op1=ALU.mult).then_inc(y_cen, 1)
                dve.wait_ge(y_std, T + 1)
                nc.vector.reciprocal(rstd[:, :], std[:, :]).then_inc(y_rstd, 1)
                dve.wait_ge(y_rstd, T + 1)
                dve.wait_ge(y_cen, T + 1)
                nc.vector.scalar_tensor_tensor(out=z_sb[:, i, :], in0=z_sb[:, i, :], scalar=rstd[:, :],
                                               in1=beta_b[:, :], op0=ALU.mult, op1=ALU.add).then_inc(z_done, 1)

            def batch_rows(b, more):
                for lt in range(LT):
                    if more:
                        norm(b + 1, 2 * lt)
                        norm(b + 1, 2 * lt + 1)
                    rows(b, lt)

            batch_rows(0, True)
            dve.wait_ge(r_in, 32)
            nc.vector.reciprocal(sums[:, EARLY:], sums[:, EARLY:]).then_inc(r_done, 1)
            with dve.Fori(1, NB - 1) as b:
                batch_rows(b, True)
            batch_rows(NB - 1, False)

        @block.tensor
        def _(pe):
            pe.wait_ge(consts_ready, 6)

            def do(t, g, e):
                kind = e[0]
                if kind == "x_turn":
                    src, d = e[1], e[2]
                    pe.wait_ge(x_in[d % 2], 16 * (8 * (t + 1) + 4 * src + d // 2 + 1))
                    bank_free(t, g, e)
                    for a in range(LT):
                        mm = nc.tensor.transpose(S[e[-2]][:, a * P:(a + 1) * P],
                                                 x_raw[:, d % 2, a * P:(a + 1) * P], ident[:, :])
                    mm.then_inc(x_turned, 1)
                elif kind == "mm":
                    m, a, b = e[1], e[2], e[3]
                    c = m % 2
                    col = D + m * P if m < 4 else (m - 4) * P
                    if a == 0:
                        if isinstance(t, int) and t == -1 and m == 4:
                            pe.wait_ge(w_lo_done, 24)
                        wait(pe, c_free[c], tile_no(t, m) - 1)
                    if m in (0, 4):
                        if isinstance(t, int) and t == -1 and m == 0:
                            pe.wait_ge(w_lo_done, a // 3 + 1)
                        pe.wait_ge(x_lo_done, x_no(t, m // 4, a // 3))
                    for n in range(a, b):
                        d, part = n // 3, n % 3
                        w = (w_lo, w_hi, w_hi)[part]
                        xx = (xT_hi, xT_lo, xT_hi)[part]
                        mm = nc.tensor.matmul(C[c][:, :], w[:, d, col:col + P], xx[:, d, :],
                                              start=(n == 0), stop=(n == 23))
                    if b == 24:
                        mm.then_inc(c_full[c], 1)
                elif kind == "v_turn":
                    j = e[1]
                    bank_free(t, g, e)
                    pe.wait_ge(c_free[j % 2], tile_no(t - 1, 2 + j))
                    for s in range(ST):
                        mm = nc.tensor.transpose(S[e[2]][:, s * P:(s + 1) * P], vT_sb[:, j, s * P:(s + 1) * P],
                                                 ident[:, :])
                    mm.then_inc(v_turned, 1)
                elif kind == "mask_turn":
                    st = e[1]
                    if st == 0:
                        pe.wait_ge(mask_in, 16 * (t + 2))
                    bank_free(t, g, e)
                    for a in range(LT):
                        mm = nc.tensor.transpose(S[e[-2]][:, a * P:(a + 1) * P],
                                                 mask_l[:, a, st * P:(st + 1) * P], ident[:, :])
                    mm.then_inc(mask_turned, 1)
                elif kind == "shift_turn":
                    G = group(t, g) + 1
                    bank_free(t, g, e)
                    pe.wait_ge(neg_lo, G + 1)
                    nc.tensor.transpose(S[e[1]][0:32, 0:P], shift[:, :].bitcast(F32), ident[:, :])\
                      .then_inc(shift_turned, 1)
                elif kind == "p1":
                    i = e[1]
                    b = (g + 1) % 2
                    h, lt = i // 4, i % 4
                    if i == 0:
                        pe.wait_ge(stack_in, 96 * (group(t, g) + 2))
                    bank_free(t, g, e)
                    nc.tensor.matmul(S[e[2]][:, :], q_stack[b][0:96, h, lt * P:(lt + 1) * P], k_stack[b][0:96, :],
                                     start=True, stop=True).then_inc(p1_done, 1)
                elif kind == "p2":
                    i = e[1]
                    b = g % 2
                    st, h = i // 4, i % 4
                    if i == 0:
                        pe.wait_ge(shift_in, 32 * (group(t, g) + 1))
                    bank_free(t, g, e)
                    nc.tensor.matmul(S[e[2]][:, :], k_stack[b][0:98, st * P:(st + 1) * P], q_stack[b][0:98, h, :],
                                     start=True, stop=True).then_inc(p2_done, 1)
                elif kind == "y":
                    first_rows(e[1])
                elif kind == "pv":
                    pv(t, group(t, g), g, e[1])
                elif kind == "sums_before" and not first(t, g):
                    bank_free(t, g, e)
                    sums_over_keys(group(t, g) - 1, e[1])
                elif kind == "pv_before" and not first(t, g):
                    pv(t, group(t, g) - 1, (g - 1) % NG, 3)

            def products(y, d_hi, d_lo, k, lt, c):
                for n, (o, w) in enumerate(((d_hi, w_lo), (d_lo, w_hi), (d_hi, w_hi))):
                    mm = nc.tensor.matmul(y[:, :], o[:, k, lt * P:(lt + 1) * P], w[:, k, c * 512:(c + 1) * 512],
                                          start=(k == 0 and n == 0), stop=(k == KD - 1 and n == 2))
                return mm

            def first_rows(k):
                if k == 0:
                    pe.wait_ge(wo_lo_done, 16)
                    for c in range(2):
                        pe.wait_ge(c_free[c], tile_no(NB - 2, 10 + c))
                pe.wait_ge(on_lo, k + 1)
                for c in range(2):
                    mm = products(Y[c], *halves(0), k, 0, c)
                    if k == KD - 1:
                        mm.then_inc(y_full, 1)

            def bank_free(t, g, e):
                if e[-1] is None:
                    return
                had, back = e[-1]
                if back:
                    t, g = (t, g - 1) if g > 0 else (t - 1, NG - 1)
                G = group(t, g)
                if had[0] == "p1":
                    pe.wait_ge(max_done, 16 * (G + 1) + had[1] + 1)
                elif had[0] == "p2":
                    pe.wait_ge(exp_done, 16 * G + had[1] + 1)
                elif had[0] == "x_turn":
                    pe.wait_ge(x_lo_done, x_no(t, had[1], had[2]))
                elif had[0] == "mask_turn":
                    pe.wait_ge(mask_out, 4 * (t + 1 if g == NG - 1 else t) + had[1] + 1)
                elif had[0] == "v_turn":
                    pe.wait_ge(v_out, 2 * t + had[1] + 1)
                elif had[0] == "shift_turn":
                    pe.wait_ge(shift_out, G + 2)
                else:
                    pe.wait_ge(r_out, G)

            def pv(t, G, g, st):
                pe.wait_ge(exp_done, 16 * G + 4 * st + 4)
                if st == 0:
                    wait(pe, o_out, G)
                    if g == 0:
                        pe.wait_ge(v_out, 2 * t + 2)
                for h in range(GH):
                    mm = nc.tensor.matmul(O_ps[HD * h:HD * (h + 1), :], v_sb[:, st, HD * g:HD * (g + 1)],
                                          probs[:, 4 * (st % 2) + h, :], start=(st == 0), stop=(st == ST - 1))
                mm.then_inc(pv_done, 1)

            def sums_over_keys(G, bank_no):
                pe.wait_ge(acc_done, 12 * (G + 1))
                for h in range(GH):
                    mm = nc.tensor.matmul(S[bank_no][HD * h:HD * (h + 1), :], ones[:, :], acc[:, h, :],
                                          start=True, stop=True)
                mm.then_inc(sum_done, 1)

            walk(pe, do)
            pv(NB - 1, NB * NG - 1, NG - 1, 3)
            pe.wait_ge(exp_done, 16 * NG * NB)
            sums_over_keys(NB * NG - 1, AFTER[-2][1])

            for k in range(sum(e[0] == "y" for e in LAST[-1]), KD):
                first_rows(k)

            def rows(b, lt, odd):
                d_hi, d_lo = halves(odd)
                T = LT * b + lt
                i = lt % 2
                for c in range(2):
                    if not (isinstance(b, int) and b == 0 and lt < 2):
                        pe.wait_ge(y_added, 2 * (T - 2) + c + 1)
                    for k in range(KD):
                        mm = products(Y[2 * i + c], d_hi, d_lo, k, lt, c)
                    mm.then_inc(y_full, 1)

            def batch_rows(b, odd):
                pe.wait_ge(on_lo, NG * (b + 1))
                for lt in range(LT):
                    rows(b, lt, odd)

            for lt in range(1, LT):
                rows(0, lt, 0)
            batch_rows(1, 1)
            with pe.Fori(1, NB // 2) as p:
                batch_rows(2 * p, 0)
                batch_rows(2 * p + 1, 1)


_INS = ["x", "ctx_2048", "mask_Bx1xSxS2_ff0", "L0_xattn_Wq", "L0_xattn_bq", "L0_xattn_Wk", "L0_xattn_bk",
        "L0_xattn_Wv", "L0_xattn_bv", "L0_xattn_Wo", "L0_xattn_bo", "L0_xattn_gamma", "L0_xattn_beta"]


def kernel(**inputs):
    import numpy as _np
    import concourse.bacc as _bacc
    from concourse import mybir as _mybir
    from concourse.bass_utils import run_bass_kernel_spmd as _run

    nc = _bacc.Bacc("TRN2", target_bir_lowering=False, num_devices=1)
    arrays, args = {}, []
    for name in _INS:
        a = _np.ascontiguousarray(inputs[name])
        arrays[f"in_{name}_dram"] = a
        args.append(nc.dram_tensor(f"in_{name}_dram", a.shape, _mybir.dt.from_np(a.dtype), kind="ExternalInput").ap())
    shape = inputs["x"].shape
    args.append(nc.dram_tensor("out_0_dram", shape, _mybir.dt.float32, kind="ExternalOutput").ap())
    attention_kernel(nc, *args)
    r = _run(nc, [arrays], core_ids=[0])
    return r.results[0]["out_0_dram"]
```
